# Optimizing a Trainium2 kernel written in Bass

```python
import numpy as np
import jax
import jax.numpy as jnp

def _softmax(x, axis=-1):
    return jax.nn.softmax(x, axis=axis)
def _gelu(x):
    return jax.nn.gelu(x, approximate=True)
def _silu(x):
    return jax.nn.silu(x)
def _sigmoid(x):
    return jax.nn.sigmoid(x)
def _layernorm(x, axis=-1, eps=1e-5):
    m = jnp.mean(x, axis=axis, keepdims=True)
    v = jnp.var(x, axis=axis, keepdims=True)
    return (x - m) / jnp.sqrt(v + eps)
def _scatter_add(tgt, idx, src, axis=0):
    return tgt.at[idx].add(src)
def _segment_sum(src, seg, n):
    return jax.ops.segment_sum(src, seg, n)

kernel_name = 'mk_conv_preact_d2_conv_nchw256_618250'

def setup_inputs(seed: int = 0):
    np.random.seed(seed)
    _w = jnp.asarray
    def _rec_inputs():
        import jax
        import jax.numpy as jnp
        _gk = jax.random.key(seed)
        x = -0.0002928 + 1 * jax.random.normal(jax.random.fold_in(_gk, 1), (4, 256, 64, 64), jnp.float32)
        return x
    x = _rec_inputs()
    def _L0_conv_setup():
        import jax, jax.numpy as jnp
        import numpy as np
        from jax import lax
        B, C, H, W = (4, 256, 64, 64)
        C8 = C // 8
        key = jax.random.key(seed)
        ks = jax.random.split(key, 8)
        x = jax.random.normal(ks[0], (B, C, H, W), jnp.float32)
        wb = jax.random.normal(ks[1], (C8, 2 * C), jnp.float32) * 0.02
        bb = jax.random.normal(ks[2], (C8,), jnp.float32) * 0.02
        wc = jax.random.normal(ks[3], (C8, 2 * C), jnp.float32) * 0.02
        bc = jax.random.normal(ks[4], (C8,), jnp.float32) * 0.02
        wd = jax.random.normal(ks[5], (C, 2 * C), jnp.float32) * 0.02
        bd = jax.random.normal(ks[6], (C,), jnp.float32) * 0.02
        alpha = jnp.float32(0.5)
        return {'x': x, 'wb': wb, 'bb': bb, 'wc': wc, 'bc': bc, 'wd': wd, 'bd': bd, 'alpha': alpha}
    _L0_conv_all = _L0_conv_setup()
    _L0_conv_in = {k: v for k, v in _L0_conv_all.items() if k in ('wb', 'bb', 'wc', 'bc', 'wd', 'bd', 'alpha', )}
    del _L0_conv_all

    def _L1_conv_setup():
        import jax, jax.numpy as jnp
        import numpy as np
        from jax import lax
        DN = ('NCHW', 'OIHW', 'NCHW')

        def _dwconv(x, w, b, pad):
            y = lax.conv_general_dilated(x, w, (1, 1), [(pad, pad), (pad, pad)], feature_group_count=x.shape[1], dimension_numbers=DN)
            return y + b[None, :, None, None]

        def _mish(x):
            return x * jnp.tanh(jax.nn.softplus(x))
        key = jax.random.key(seed)
        ks = jax.random.split(key, 16)
        B, C, H, W = (32, 256, 64, 64)
        Cr = C // 4
        s = 0.05
        return {'x': jax.random.normal(ks[0], (B, C, H, W), jnp.float32), 'w3': jax.random.normal(ks[1], (C, 1, 3, 3), jnp.float32) * s, 'b3': jax.random.normal(ks[2], (C,), jnp.float32) * s, 'w5': jax.random.normal(ks[3], (C, 1, 5, 5), jnp.float32) * s, 'b5': jax.random.normal(ks[4], (C,), jnp.float32) * s, 'w7': jax.random.normal(ks[5], (C, 1, 7, 7), jnp.float32) * s, 'b7': jax.random.normal(ks[6], (C,), jnp.float32) * s, 'w_pw': jax.random.normal(ks[7], (C, 3 * C), jnp.float32) * s, 'b_pw': jax.random.normal(ks[8], (C,), jnp.float32) * s, 'w_a1': jax.random.normal(ks[9], (Cr, C), jnp.float32) * s, 'b_a1': jax.random.normal(ks[10], (Cr,), jnp.float32) * s, 'w_a2': jax.random.normal(ks[11], (3, Cr), jnp.float32) * s, 'b_a2': jax.random.normal(ks[12], (3,), jnp.float32) * s}
    _L1_conv_all = _L1_conv_setup()
    _L1_conv_in = {k: v for k, v in _L1_conv_all.items() if k in ('w3', 'b3', 'w5', 'b5', 'w7', 'b7', 'w_pw', 'b_pw', 'w_a1', 'b_a1', 'w_a2', 'b_a2', )}
    del _L1_conv_all

    return {
        "x": x,
        "L0_conv_wb": _L0_conv_in["wb"],
        "L0_conv_bb": _L0_conv_in["bb"],
        "L0_conv_wc": _L0_conv_in["wc"],
        "L0_conv_bc": _L0_conv_in["bc"],
        "L0_conv_wd": _L0_conv_in["wd"],
        "L0_conv_bd": _L0_conv_in["bd"],
        "L0_conv_alpha": _L0_conv_in["alpha"],
        "L1_conv_w3": _L1_conv_in["w3"],
        "L1_conv_b3": _L1_conv_in["b3"],
        "L1_conv_w5": _L1_conv_in["w5"],
        "L1_conv_b5": _L1_conv_in["b5"],
        "L1_conv_w7": _L1_conv_in["w7"],
        "L1_conv_b7": _L1_conv_in["b7"],
        "L1_conv_w_pw": _L1_conv_in["w_pw"],
        "L1_conv_b_pw": _L1_conv_in["b_pw"],
        "L1_conv_w_a1": _L1_conv_in["w_a1"],
        "L1_conv_b_a1": _L1_conv_in["b_a1"],
        "L1_conv_w_a2": _L1_conv_in["w_a2"],
        "L1_conv_b_a2": _L1_conv_in["b_a2"],
    }

def reference(x, L0_conv_wb, L0_conv_bb, L0_conv_wc, L0_conv_bc, L0_conv_wd, L0_conv_bd, L0_conv_alpha, L1_conv_w3, L1_conv_b3, L1_conv_w5, L1_conv_b5, L1_conv_w7, L1_conv_b7, L1_conv_w_pw, L1_conv_b_pw, L1_conv_w_a1, L1_conv_b_a1, L1_conv_w_a2, L1_conv_b_a2):
    import jax
    import jax.numpy as jnp
    def _L0_conv_ref(x, wb, bb, wc, bc, wd, bd, alpha):
        import jax, jax.numpy as jnp
        import numpy as np
        from jax import lax
        B, C, H, W = (4, 256, 64, 64)
        C8 = C // 8
        b, c, h, w = x.shape
        n = h * w
        pad = [(0, 0), (0, 0), (1, 1), (1, 1)]
        x_avg = lax.reduce_window(x, 0.0, lax.add, (1, 1, 3, 3), (1, 1, 1, 1), pad) / 9.0
        x_max = lax.reduce_window(x, -jnp.inf, lax.max, (1, 1, 3, 3), (1, 1, 1, 1), pad)
        cat = jnp.concatenate([x_avg, x_max], axis=1)
        catf = cat.reshape(b, 2 * c, n)
        feat_b = jnp.einsum('oc,bcn->bon', wb, catf) + bb[None, :, None]
        feat_c = jnp.einsum('oc,bcn->bon', wc, catf) + bc[None, :, None]
        feat_d = jnp.einsum('oc,bcn->bon', wd, catf) + bd[None, :, None]
        attn = jax.nn.softmax(jnp.einsum('bon,bom->bnm', feat_b, feat_c), axis=-1)
        feat_e = jnp.einsum('bcn,bmn->bcm', feat_d, attn).reshape(b, c, h, w)
        return alpha * feat_e + (1.0 - alpha) * x

    def _L1_conv_ref(x, w3, b3, w5, b5, w7, b7, w_pw, b_pw, w_a1, b_a1, w_a2, b_a2):
        import jax, jax.numpy as jnp
        import numpy as np
        from jax import lax
        DN = ('NCHW', 'OIHW', 'NCHW')

        def _dwconv(x, w, b, pad):
            y = lax.conv_general_dilated(x, w, (1, 1), [(pad, pad), (pad, pad)], feature_group_count=x.shape[1], dimension_numbers=DN)
            return y + b[None, :, None, None]

        def _mish(x):
            return x * jnp.tanh(jax.nn.softplus(x))
        x3 = _dwconv(x, w3, b3, 1)
        x5 = _dwconv(x, w5, b5, 2)
        x7 = _dwconv(x, w7, b7, 3)
        x_cat = jnp.concatenate([x3, x5, x7], axis=1)
        x_out = jnp.einsum('bchw,oc->bohw', x_cat, w_pw) + b_pw[None, :, None, None]
        g = jnp.mean(x_out, axis=(2, 3))
        h = _mish(g @ w_a1.T + b_a1)
        logits = h @ w_a2.T + b_a2
        weights = jax.nn.softmax(logits, axis=1)
        x_stack = jnp.stack([x3, x5, x7], axis=1)
        return jnp.einsum('bk,bkchw->bchw', weights, x_stack)

    def _gn(v, G=32, eps=1e-5):
        B_, C_, H_, W_ = v.shape
        g = v.reshape(B_, G, C_ // G, H_, W_)
        m = jnp.mean(g, axis=(2, 3, 4), keepdims=True)
        s = jnp.var(g, axis=(2, 3, 4), keepdims=True)
        return ((g - m) / jnp.sqrt(s + eps)).reshape(v.shape)

    def _ln_c(v, eps=1e-6):
        m = jnp.mean(v, axis=1, keepdims=True)
        s = jnp.var(v, axis=1, keepdims=True)
        return (v - m) / jnp.sqrt(s + eps)

    def _ln_t(v, eps=1e-5):
        m = jnp.mean(v, axis=-1, keepdims=True)
        s = jnp.var(v, axis=-1, keepdims=True)
        return (v - m) / jnp.sqrt(s + eps)

    def _to_tokens(v):
        B_, C_, H_, W_ = v.shape
        return v.reshape(B_, C_, H_ * W_).transpose(0, 2, 1)
    def _from_tokens(t, like):
        B_, C_, H_, W_ = like.shape
        return t.transpose(0, 2, 1).reshape(B_, C_, H_, W_)

    x = x + _L0_conv_ref(_gn(x), L0_conv_wb, L0_conv_bb, L0_conv_wc, L0_conv_bc, L0_conv_wd, L0_conv_bd, L0_conv_alpha)
    x = x + _L1_conv_ref(_gn(x), L1_conv_w3, L1_conv_b3, L1_conv_w5, L1_conv_b5, L1_conv_w7, L1_conv_b7, L1_conv_w_pw, L1_conv_b_pw, L1_conv_w_a1, L1_conv_b_a1, L1_conv_w_a2, L1_conv_b_a2)
    return x


_drawn_inputs = setup_inputs


def setup_inputs(seed=0):
    import zlib

    import numpy as np

    out = dict(_drawn_inputs(seed))
    spreads = {}
    factors = {'L0_conv_wb': 8.0,
     'L0_conv_bb': 23.682,
     'L0_conv_wc': 8.0,
     'L0_conv_bc': 64.0,
     'L0_conv_bd': 8.0,
     'L1_conv_b3': 40.96,
     'L1_conv_b5': 17.273,
     'L1_conv_b7': 4.772,
     'L1_conv_w_pw': 64.0,
     'L1_conv_b_pw': 64.0,
     'L1_conv_w_a1': 8.0,
     'L1_conv_b_a1': 64.0,
     'L1_conv_w_a2': 64.0,
     'L1_conv_b_a2': 64.0,
     'L1_conv_w3': 8.0,
     'L1_conv_w5': 8.0}
    for name, (base, spread) in spreads.items():
        noise = np.random.default_rng([zlib.crc32(name.encode()), seed]).standard_normal(out[name].shape)
        drawn = base * np.exp(spread * noise) if base else spread * noise
        out[name] = jnp.asarray(drawn.astype(out[name].dtype))
    for name, factor in factors.items():
        out[name] = (out[name] * factor).astype(out[name].dtype)
    return out
```

```python
from contextlib import ExitStack

import numpy as np

import concourse.bass as bass
from concourse import mybir

F32, F16 = mybir.dt.float32, mybir.dt.float16
ALU = mybir.AluOpType
ACT = mybir.ActivationFunctionType
X, XY = mybir.AxisListType.X, mybir.AxisListType.XY

B, C, H, W = 4, 256, 64, 64
N = H * W
P = 128
CT = C // P
C8 = C // 8
KT = 2 * CT
GN_GROUP = 8
CHUNK = 512
NCH = N // CHUNK
KEYT = N // P
NB = CHUNK // P
ROWS = CHUNK // W
GC, WIN, TO = 8, 16, 10
TAPS = 7
NT = -(-H // TO)
NG = C // GC
SEG = 2 * TAPS
ULEN = SEG * 16 + 16
MO = TO * GC
GN_MAX = 182.0
XS = 16.0
WS = 2048.0
MAXROW = 32768.0
QK_TOP = 4096.0
P_TOP = 512.0
DV_SHIFT = 2.0 ** -8
DV_SCALE = XS * WS * DV_SHIFT
KW = 256.0
EPS = 1e-5


def build(nc, x, wall, w7, wpw, wa1, wa2, cols, rows, consts, out):
    ctx = ExitStack()
    with ctx:
        def sb(name, shape, dt=F32):
            return ctx.enter_context(nc.sbuf_tensor(name, shape, dt))

        def sem(name):
            return ctx.enter_context(nc.semaphore(name))

        x1w = nc.dram_tensor("x1w", [B, C, WIN, NT, W], F32)
        kern = nc.dram_tensor("kern", [C, ULEN], F16)
        scal_in = nc.dram_tensor("scal_in", [B, GC, NG, 2], F32)
        scal_out = nc.dram_tensor("scal_out", [B, GC, NG, 2], F32)

        cst_all = sb("cst_all", [P, 2 * P + NT + GC])
        ident, gmat = cst_all[:, 0:P], cst_all[:, P:2 * P]
        cst = cst_all[:, 2 * P:]
        identh = sb("identh", [P, P], F16)
        maskc = sb("maskc", [P, GC], F16)
        ones = sb("ones", [P, P])
        wh = sb("wh", [P, KT, C + 2 * C8], F16)
        wl = sb("wl", [P, KT, C + 2 * C8], F16)
        w7s = sb("w7s", [P, CT, 3, 49])
        wpws = sb("wpws", [P, 3 * CT, C])
        wa1s = sb("wa1s", [P, CT, 64])
        wa2s = sb("wa2s", [64, 3])
        col = sb("col", [P, 12])
        row = sb("row", [P, 64 + 3 + 1 + 49])
        BD, BPW, DWB, BBC, BA1 = 0, 2, 4, 10, 11
        bbrow, ba2r, alpha, cnt = row[:, 0:64], row[:, 64:67], row[:, 67:68], row[:, 68:117]

        small = sb("small", [P, 16])
        escale = sb("escale", [P, 1])
        lnp = sb("lnp", [P, 1])
        epst = sb("epst", [P, 1])
        qk_scale = sb("qk_scale", [64, 1])
        qk_bias = sb("qk_bias", [64, 1])
        vdesc = sb("vdesc", [P, CT])
        xin = sb("xin", [P, 2, CT, CHUNK])
        st0 = sb("st0", [P, B, NCH, CT, 6])
        me0 = sb("me0", [P, B * CT, 2])
        gn0 = sb("gn0", [P, 8, B * CT])
        gnp = sb("gnp", [P, B, CT, 4])

        hx = sb("hx", [P, CT, ROWS + 2, W])
        gcur = sb("gcur", [P, CT, 2])
        pairs = [sb(f"pairs_{o}", [P, CT, (ROWS + 1) * W]) for o in ("sum", "max")]
        threes = [sb(f"threes_{o}", [P, CT, ROWS, W + 2]) for o in ("sum", "max")]
        pooled = [sb(f"pooled_{o}", [P, CT, CHUNK]) for o in ("sum", "max")]
        cath = sb("cath", [P, KT, N], F16)
        catl = sb("catl", [P, KT, N], F16)

        vh = sb("vh", [P, KEYT, C + 2], F16)
        vl = sb("vl", [P, KEYT, C], F16)
        bq = sb("bq", [P, N], F16)
        ck = sb("ck", [P, N], F16)
        qk32 = sb("qk32", [64, CHUNK])
        pbuf = sb("pbuf", [P, 4, 2 * CHUNK])
        p32 = [pbuf[:, i, 0:CHUNK] for i in range(4)]
        ph = [pbuf[:, i, CHUNK:CHUNK + 256].bitcast(F16) for i in range(4)]
        pl = [pbuf[:, i, CHUNK + 256:2 * CHUNK].bitcast(F16) for i in range(4)]
        flatp = pbuf[:].rearrange("p a b -> p (a b)")
        NW = C + 2 * C8
        wraw = flatp[:, 0:KT * NW].rearrange("p (k n) -> p k n", k=KT)
        wabs = flatp[:, KT * NW:2 * KT * NW].rearrange("p (k n) -> p k n", k=KT)
        wtot = flatp[:, 2 * KT * NW:(2 * KT + 1) * NW]
        wscale = flatp[:, (2 * KT + 1) * NW:(2 * KT + 2) * NW]
        mx = sb("mx", [P, NB, NCH])
        nmax = sb("nmax", [P, NB])
        m2 = sb("m2", [P, NB, 2], F16)
        rden = sb("rden", [P, NB])
        obuf = sb("obuf", [P, NB * C + CT * CHUNK])
        onorm = obuf[:, 0:NB * C].rearrange("p (a b) -> p a b", b=C)
        x1c = obuf[:, NB * C:].rearrange("p (t n) -> p t n", n=CHUNK)
        halo = CT * (ROWS + 2) * W
        zeros = obuf[:, 0:NB * C + CT * CHUNK - halo]
        hxs = [hx, obuf[:, NB * C + CT * CHUNK - halo:].rearrange("p (t r w) -> p t r w", t=CT, w=W)]
        xw = xin[:, 0].rearrange("p t n -> p (t n)")[:, 0:2 * NT * W].rearrange("p (u t w) -> p u t w", u=2, w=W)
        xgh, xgl = (onorm.rearrange("p a b -> p (a b)")[:, i * NT * W:(i + 1) * NT * W].bitcast(F16)
                    .rearrange("p (u t w) -> p u t w", u=2, w=W) for i in range(2))
        xg = x1c[:, 0, 0:NT * W].rearrange("p (t w) -> p t w", w=W)
        yo = xin[0:MO, 1].rearrange("p t n -> p (t n)")[:, 0:2 * NT * W].rearrange("p (u t w) -> p u t w", u=2, w=W)

        st1 = sb("st1", [P, CT, NCH, 6])
        rsum = sb("rsum", [P, CT, H])
        edge = sb("edge", [P, CT, H, 6])
        acol = onorm.rearrange("p a b -> p (a b)")[:, 0:CT * 7 * H].rearrange("p (t d h) -> p t d h", t=CT, d=7)
        wsum = sb("wsum", [P, CT, 7, 7])
        l1 = sb("l1", [P, 64])
        wk = sb("wk", [P, CT, 49])
        tmpw = sb("tmpw", [P, CT, 3, 49])
        uker = sb("uker", [P, CT, ULEN], F16)
        svec = sb("svec", [P, CT, 4])
        hbc = sb("hbc", [64, P])

        vker = flatp[:, 0:NG * SEG * 16 // 2].bitcast(F16)\
            .rearrange("p (g q j) -> p g q j", g=NG, q=SEG)
        sin = sb("sin", [P, NG, 2])
        sout = sb("sout", [MO, NG, 2])
        mrow = sb("mrow", [P, NG, NT])
        tmat = sb("tmat", [P, 2, SEG, TO, GC], F16)

        bank = [ctx.enter_context(nc.psum_tensor(f"bank{i}", [P, CHUNK], F32)) for i in range(8)]
        acc, sT, aux, tiny = bank[0:4], bank[4:6], bank[6:8], bank[5]

        s_load = sem("constants_loaded")
        s_wload = sem("projection_weights_loaded")
        s_lload = sem("layer1_weights_loaded")
        s_part = sem("waits_parted")
        s_zero = sem("scratch_pads_zeroed")
        s_set = sem("setup_chain")
        s_setp = sem("setup_product_ready")
        s_seta = sem("setup_activation_ready")
        s_xin = [sem("stat_chunk_loaded_even"), sem("stat_chunk_loaded_odd")]
        s_xfree = sem("stat_chunk_free")
        s_poolset = sem("pool_setup")
        s_hx = [sem("halo_rows_loaded"), sem("halo_rows_loaded_odd")]
        s_high = sem("first_pools_high_ready")
        s_maxlow = sem("first_pools_max_low_ready")
        s_norm = sem("halo_rows_normalised")
        s_maxp = sem("pooled_maxima_ready")
        s_maxc = sem("pooled_maxima_chain")
        s_gcur = sem("pool_scalars_copied")
        s_pool = sem("pool_chain")
        s_cat = sem("pooled_rows_ready")
        s_qkps = sem("query_key_product_ready")
        s_qk32 = sem("query_key_scaled")
        s_qkh = sem("query_key_high_ready")
        s_qk = sem("query_key_low_ready")
        s_vps = sem("value_product_ready")
        s_vhi = sem("value_high_ready")
        s_vlo = sem("value_low_ready")
        s_mps = sem("max_scores_ready")
        s_mfree = sem("max_scores_reduced")
        s_mchain = sem("row_maxima_chain")
        s_m2 = sem("row_maxima_ready")
        s_mrow = sem("row_maxima_turned")
        s_rows = sem("maxima_rows_stored")
        s_st = sem("scores_ready")
        s_exp = sem("exp_ready")
        s_lo = sem("exp_low_ready")
        s_pv = sem("value_step_done")
        s_acc = sem("sum_block_done")
        s_rden = sem("reciprocal_ready")
        s_on = sem("sum_block_normalised")
        s_turn = sem("outputs_turned")
        s_xr = sem("residual_loaded")
        s_xk = sem("residual_scaled")
        s_x1 = sem("x1_chunk_ready")
        s_x1o = sem("x1_chunk_stored")
        s_x1st = sem("x1_statistics_done")
        s_l1 = sem("layer1_chain")
        s_l1p = sem("layer1_product_ready")
        s_l1a = sem("layer1_activation_ready")
        s_usto = sem("kernels_stored")
        s_uld = sem("kernels_loaded")
        s_mr = sem("window_scales_ready")
        s_xw = [sem("window_rows_loaded_even"), sem("window_rows_loaded_odd")]
        s_xg = sem("window_normalised")
        s_xgh = sem("window_high_ready")
        s_xgl = sem("window_low_ready")
        s_tm = sem("band_matrices_ready")
        s_cv = sem("convolution_ready")
        s_y = sem("output_tile_ready")
        s_out = [sem("outputs_stored_even"), sem("outputs_stored_odd")]
        s_outp = [sem("outputs_stored_by_pool_even"), sem("outputs_stored_by_pool_odd")]

        block = ctx.enter_context(nc.Block())
        ts, ds = bass.ts, bass.ds

        def part(eng):
            eng.sem_inc(s_part, 1)

        def chain(eng, s, start, parted=False):
            def link(ins):
                link.count += 1
                ins.then_inc(s, 1)
                eng.wait_ge(s, start + link.count)
                if parted:
                    part(eng)
            link.count = 0
            return link

        N_SUM, N_MAX = 7, 3
        N_SUM0 = 4
        N_L1 = 60
        hops = {}
        pieces = [[(t, max(ROWS * g, TO * t - 3), min(ROWS * g + ROWS, TO * t - 3 + WIN)) for t in range(NT)
                   if max(ROWS * g, TO * t - 3) < min(ROWS * g + ROWS, TO * t - 3 + WIN)] for g in range(NCH)]
        stores = [CT * sum(len(p) for p in pieces[:g]) for g in range(NCH + 1)]
        U_LOADS = WIN + 2
        Y_STORES = NT
        SP_STORES = 4
        POOL_STORES = Y_STORES - SP_STORES
        MAXSTEPS = NB * NCH

        xv = x.rearrange("b (t p) n -> b p t n", p=P)

        def first_image(eng, body):
            body(0, 0, 1, 0)
            with eng.Fori(0, NCH // 2 - 1) as h:
                body(h, 1, 0, 0)
                body(h + 1, 0, 0, 0)
            body(NCH // 2 - 1, 1, 0, 1)

        def stat_chunk(pair, odd, image):
            k = (B - 1) * odd + image - 1
            return k % 2, (B - 1) * pair + k // 2 + 1 + NCH // 2, 2 * (B - 1) * pair + k + 1 + NCH

        def windows(link, eng, op, kind, first, last, hx=hx):
            n = ROWS + 2 - first - last
            two = pairs[kind][:, :, 0:(n - 1) * W].rearrange("p t (r w) -> p t r w", w=W)
            cols2 = pairs[kind][:, :, 0:ROWS * (W + 1)].rearrange("p t (r w) -> p t r w", w=W + 1)
            three = threes[kind]
            inner = three[:, :, :, 1:W + 1]
            link(eng.tensor_tensor(two, hx[:, :, 0:n - 1, :], hx[:, :, 1:n, :], op))
            if first:
                link(eng.tensor_copy(inner[:, :, 0, :], two[:, :, 0, :]))
            if last:
                link(eng.tensor_copy(inner[:, :, ROWS - 1, :], two[:, :, n - 2, :]))
            link(eng.tensor_tensor(inner[:, :, first:first + n - 2, :], two[:, :, 0:n - 2, :], hx[:, :, 2:n, :], op))
            link(eng.tensor_tensor(cols2, three[:, :, :, 0:W + 1], three[:, :, :, 1:W + 2], op))
            ins = eng.tensor_tensor(pooled[kind][:].rearrange("p t (r w) -> p t r w", w=W),
                                    cols2[:, :, :, 0:W], three[:, :, :, 2:W + 2], op)
            if kind == 0:
                link(ins)
            return ins

        def store_y(eng, b, gi, u, some, s_stored):
            eng.wait_ge(s_y, 2 + b * NG + gi + 1)
            for t in some:
                m = min(TO, H - TO * t)
                eng.dma_start(bass.AP(out.tensor, b * (C * N) + gi * (GC * N) + t * TO * W,
                                      [[W, m], [N, GC], [1, W]]),
                              yo[0:m * GC, u, t, :]).then_inc(s_stored[u], 16)

        @block.vector
        def _(dve):
            V = nc.vector
            link = chain(dve, s_set, 0)
            V.memset(lnp[:], float(np.log(P_TOP))).then_inc(s_pv, 4)
            V.memset(epst[:], EPS).then_inc(s_xfree, 2)
            V.memset(m2[:], 0.0).then_inc(s_vlo, 4)
            V.memset(mx[:], 0.0).then_inc(s_mfree, 2)
            V.memset(uker[:], 0.0).then_inc(s_cv, 2)
            V.memset(nmax[:], 0.0).then_inc(s_y, 2)
            link(V.memset(zeros, 0.0))
            hops["zeros"] = link.count
            link(V.memset(ones[:], 1.0))
            link(V.memset(threes[1][:], -3.0e38))
            link(V.memset(ck[96:98, :], MAXROW))
            link(V.memset(vh[:, :, C:C + 1], 1.0))

            def image_statistics(b0, b1):
                for b in range(b0, b1):
                    for t in range(CT):
                        link(V.bn_aggr(me0[:, b * CT + t, :], st0[:, b, :, t, :]))
                some = slice(b0 * CT, b1 * CT)
                link(V.tensor_tensor(gn0[:, 0, some], me0[:, some, 0], me0[:, some, 0], ALU.mult))
                link(V.tensor_tensor(me0[:, some, 1], me0[:, some, 1], gn0[:, 0, some], ALU.add))
                hops["me0", b0] = link.count

            def image_scalars(b0, b1, turn):
                some = slice(b0 * CT, b1 * CT)
                gsum = tiny[:, 0:2 * B * CT].rearrange("p (i v) -> p i v", v=2)
                link(V.tensor_copy(gn0[:, 1, some], gsum[:, some, 0]))
                link(V.tensor_tensor(gn0[:, 2, some], gn0[:, 1, some], gn0[:, 1, some], ALU.mult))
                link(V.tensor_tensor(gn0[:, 3, some], gsum[:, some, 1], gn0[:, 2, some], ALU.subtract))
                hops["var0", b0] = link.count
                dve.wait_ge(s_seta, turn)
                link(V.reciprocal(gn0[:, 5, some], gn0[:, 4, some]))
                r0, mean0 = gn0[:, 5, some], gn0[:, 1, some]
                flat = gnp[:].rearrange("p b t v -> p (b t) v")[:, some]
                link(V.tensor_scalar(flat[:, :, 0], r0, XS, None, ALU.mult))
                link(V.scalar_tensor_tensor(flat[:, :, 1], mean0, -XS, r0, ALU.mult, ALU.mult))
                hops["gnp", b0] = link.count
                link(V.tensor_scalar(flat[:, :, 2], r0, small[:, 8:9], 1.0, ALU.mult, ALU.add))
                link(V.scalar_tensor_tensor(gn0[:, 6, some], mean0, small[:, 8:9], r0, ALU.mult, ALU.mult))
                for t in range(CT):
                    link(V.tensor_scalar(gnp[:, b0:b1, t, 3],
                                         gn0[:, 6, some].rearrange("p (b t) -> p t b", t=CT)[:, t, :],
                                         -1.0, small[:, 9 + t:10 + t], ALU.mult, ALU.add))

            with dve.Fori(0, NCH // 2) as h:
                for u in range(2):
                    dve.wait_ge(s_xin[u], 16 * (h + 1))
                    for t in range(CT):
                        ins = V.bn_stats(st0[:, 0, h * 2 + u, t, :], xin[:, u, t, :])
                    ins.then_inc(s_xfree, 1)
            dve.wait_ge(s_xfree, 2 + NCH)
            dve.wait_ge(s_load, 16 * 3)
            link(V.tensor_scalar(small[:, 8:9], alpha, -1.0, 1.0, ALU.mult, ALU.add))
            link(V.tensor_scalar(small[:, 9:11], col[:, BD:BD + CT], alpha, None, ALU.mult))
            image_statistics(0, 1)
            dve.wait_ge(s_setp, 1)
            image_scalars(0, 1, 1)

            def set_up_weights():
                dve.wait_ge(s_wload, 16)
                link(V.tensor_copy(identh[:], ident))
                link(V.tensor_copy(maskc[:], cst[:, NT:NT + GC]))
                link(V.scalar_tensor_tensor(wabs, wraw, -1.0, wraw, ALU.mult, ALU.max))
                hops["wabs"] = link.count
                dve.wait_ge(s_setp, 2)
                link(V.tensor_scalar(wtot, bank[0][:, 0:C + 2 * C8], 1e-30, None, ALU.max))
                hops["wtot"] = link.count
                for i in range(2):
                    span = wtot[:, C + i * C8:C + (i + 1) * C8]
                    link(V.tensor_reduce(small[:, i:i + 1], span, X, ALU.max))
                    link(V.tensor_scalar(span, span, 0.0, small[:, i:i + 1], ALU.mult, ALU.add))
                    link(V.tensor_reduce(small[:, 2 + i:3 + i], bbrow[:, i * C8:(i + 1) * C8], X, ALU.max,
                                         apply_absolute_value=True))
                    link(V.scalar_tensor_tensor(small[:, 4 + i:5 + i], small[:, i:i + 1], GN_MAX,
                                                small[:, 2 + i:3 + i], ALU.mult, ALU.add))
                    link(V.reciprocal(small[:, 6 + i:7 + i], small[:, 4 + i:5 + i]))
                    q = slice(i * C8, (i + 1) * C8)
                    link(V.scalar_tensor_tensor(qk_scale[q], small[q, i:i + 1], QK_TOP / (XS * WS),
                                                small[q, 6 + i:7 + i], ALU.mult, ALU.mult))
                    link(V.scalar_tensor_tensor(qk_bias[q], col[q, BBC:BBC + 1], QK_TOP,
                                                small[q, 6 + i:7 + i], ALU.mult, ALU.mult))
                link(V.scalar_tensor_tensor(escale[:], small[:, 4:5], QK_TOP ** -2, small[:, 5:6],
                                            ALU.mult, ALU.mult))
                link(V.reciprocal(wscale, wtot))
                for k in range(KT):
                    link(V.scalar_tensor_tensor(wabs[:, k, :], wraw[:, k, :], WS / 9.0 if k < CT else WS,
                                                wscale, ALU.mult, ALU.mult))
                link(V.tensor_copy(wh[:], wabs))
                link(V.tensor_tensor(wl[:], wabs, wh[:], ALU.subtract))
                hops["weights"] = link.count
                dve.wait_ge(s_setp, 3)
                link(V.tensor_scalar(vdesc[:], bank[1][:, 0:CT], alpha, 1.0 / DV_SCALE, ALU.mult, ALU.mult))
                hops["vdesc"] = link.count

            def pool_maxima(b, q, first, last):
                n = b * NCH + q
                dve.wait_ge(s_norm, CT * (n + 1))
                dve.wait_ge(s_cat, n)
                link = chain(dve, s_maxc, n * N_MAX + 2 * b + (0 if first else 1))
                windows(link, V, ALU.max, 1, first, last).then_inc(s_maxp, 1)
                assert link.count == N_MAX + first + last, link.count

            def feature_chunk(b, j):
                dve.wait_ge(s_qkh, b * NCH + j + 1)
                V.tensor_tensor(bq[32:64, ts(j, CHUNK)], qk32[0:32], bq[0:32, ts(j, CHUNK)], ALU.subtract)
                V.tensor_tensor(ck[64:96, ts(j, CHUNK)], qk32[32:64], ck[32:64, ts(j, CHUNK)],
                                ALU.subtract).then_inc(s_qk, 1)
                for u in range(4):
                    dve.wait_ge(s_vhi, b * KEYT + j * 4 + u + 1)
                    V.scalar_tensor_tensor(vl[:, j * 4 + u, :], bank[1 + u][:, 0:C], DV_SHIFT,
                                           vh[:, j * 4 + u, 0:C], ALU.mult, ALU.subtract)\
                        .then_inc(s_vlo, 1)

            def features(b):
                with dve.Fori(0, NCH) as j:
                    feature_chunk(b, j)

            def first_chunk(pair, odd, first, last):
                q = pair * 2 + odd
                dve.wait_ge(s_norm, CT * (q + 1))
                if not first:
                    dve.wait_ge(s_high, 2 * q)
                    dve.wait_ge(s_maxlow, q)
                windows(chain(dve, s_maxc, q * N_MAX + 1 - first), V, ALU.max, 1, first, last, hxs[odd])\
                    .then_inc(s_maxp, 1)
                if not first:
                    feature_chunk(0, q - 1)
                for image in range(1, B):
                    u, loads, _ = stat_chunk(pair, odd, image)
                    dve.wait_ge(s_xin[u], 16 * loads)
                    for t in range(CT):
                        ins = V.bn_stats(st0[:, image, q, t, :], xin[:, u, t, :])
                    ins.then_inc(s_xfree, 1)
                dve.wait_ge(s_maxp, q + 1)
                dve.wait_ge(s_high, 2 * q + 1)
                V.tensor_tensor(catl[:, CT:KT, ts(q, CHUNK)], pooled[1][:], cath[:, CT:KT, ts(q, CHUNK)],
                                ALU.subtract).then_inc(s_maxlow, 1)
                if first:
                    set_up_weights()

            def max_step(n, dst, e):
                dve.wait_ge(s_mps, n + 1)
                V.tensor_reduce(dst, aux[e][:], X, ALU.max).then_inc(s_mfree, 1)

            def max_pass(b):
                with dve.Fori(0, NB) as nb:
                    for c in range(NCH):
                        max_step(b * N // 16 + nb * NCH + c, mx[:, nb, c:c + 1], c % 2)

            def max_finish(r):
                dve.wait_ge(s_mfree, 2 + MAXSTEPS * (r + 1))
                dve.wait_ge(s_mrow, r)
                V.tensor_reduce(nmax[:], mx[:], X, ALU.max, negate=True).then_inc(s_mchain, 1)
                dve.wait_ge(s_mchain, 2 * r + 1)
                V.tensor_scalar(m2[:, :, 0], nmax[:], 1.0 / MAXROW, None, ALU.mult).then_inc(s_mchain, 1)
                dve.wait_ge(s_mchain, 2 * r + 2)
                V.scalar_tensor_tensor(m2[:, :, 1], nmax[:], 1.0 / MAXROW, m2[:, :, 0], ALU.mult, ALU.subtract)\
                    .then_inc(s_m2, 1)

            def low_part(s, i):
                dve.wait_ge(s_exp, s + 1)
                V.tensor_tensor(pl[i], p32[i], ph[i], ALU.subtract).then_inc(s_lo, 1)

            def finish(b, g, r):
                dve.wait_ge(s_xr, 16 * (r + 1))
                for t in range(CT):
                    V.tensor_scalar(xin[:, 0, t, :], xin[:, 0, t, :], gnp[:, b, t, 2:3], gnp[:, b, t, 3:4],
                                    ALU.mult, ALU.add).then_inc(s_xk, 1)
                dve.wait_ge(s_xk, CT * (r + 1))
                for t in range(CT):
                    dve.wait_ge(s_turn, CT * r + t + 1)
                    V.scalar_tensor_tensor(x1c[:, t, :], aux[t][:], vdesc[:, t:t + 1], xin[:, 0, t, :],
                                           ALU.mult, ALU.add).then_inc(s_x1, 1)
                dve.wait_ge(s_x1, CT * (r + 1))
                for t in range(CT):
                    V.bn_stats(st1[:, t, g, :], x1c[:, t, :])
                rows4 = x1c.rearrange("p t (r w) -> p t r w", w=W)
                V.tensor_reduce(rsum[:, :, ds(g * ROWS, ROWS)], rows4, X, ALU.add)
                V.tensor_copy(edge[:, :, ds(g * ROWS, ROWS), 0:3], rows4[:, :, :, 0:3])
                V.tensor_copy(edge[:, :, ds(g * ROWS, ROWS), 3:6], rows4[:, :, :, W - 3:W]).then_inc(s_x1st, 1)

            def group(b, g, with_finish, with_next, pool_next):
                r = b * NCH + g
                s0 = r * KEYT

                def half(i, maxima):
                    for u in range(4):
                        if maxima:
                            for e in range(2):
                                max_step((r + 1) * MAXSTEPS + i * 8 + 2 * u + e, mx[:, i, 2 * u + e:2 * u + e + 1], e)
                        low_part(s0 + i * 4 + u + 2, (u + 2) % 4)

                with dve.Fori(0, 4) as i:
                    half(i, with_next)
                if with_next:
                    max_finish(r + 1)
                if with_finish:
                    finish(b, g - 1, r - 1)
                if pool_next:
                    pool_maxima(b + 1, g, int(not with_finish), int(not with_next))
                with dve.Fori(4, 7) as i:
                    half(i, False)
                for u in range(4):
                    if u < 2 or with_next:
                        low_part(s0 + 28 + u + 2, (u + 2) % 4)
                dve.wait_ge(s_on, NB * r)
                for nb in range(NB):
                    if nb < NB - 1:
                        dve.wait_ge(s_acc, (NB - 1) * r + nb + 1)
                    else:
                        dve.wait_ge(s_pv, 4 + s0 + KEYT)
                    V.reciprocal(rden[:, nb:nb + 1], acc[nb][:, C:C + 1]).then_inc(s_rden, 1)

            def attention(b, pool_next):
                max_finish(b * NCH)
                for u in range(2):
                    low_part(b * NCH * KEYT + u, u)
                group(b, 0, False, True, pool_next)
                with dve.Fori(1, NCH - 1) as g:
                    group(b, g, True, True, pool_next)
                group(b, NCH - 1, True, False, pool_next)
                finish(b, NCH - 1, b * NCH + NCH - 1)

            def layer1(b):
                link = chain(dve, s_l1, b * N_L1)
                T, S, M, A, SUB = V.tensor_tensor, V.scalar_tensor_tensor, ALU.mult, ALU.add, ALU.subtract

                def cols(a, n=1):
                    return l1[:, a:a + n]
                dve.wait_ge(s_x1st, NCH * (b + 1))
                part(dve)
                me = cols(0, 4).rearrange("p (t v) -> p t v", v=2)
                for t in range(CT):
                    link(V.bn_aggr(me[:, t, :], st1[:, t, :, :]))
                    part(dve)
                link(T(cols(4, 2), me[:, :, 0], me[:, :, 0], M))
                link(T(me[:, :, 1], me[:, :, 1], cols(4, 2), A))
                hops["me"] = link.count
                link(V.tensor_copy(acol[:, :, 3, :], rsum[:]))
                for d, e in ((4, 0), (5, 1), (6, 2), (2, 5), (1, 4), (0, 3)):
                    near = d - 1 if d > 3 else d + 1
                    link(T(acol[:, :, d, :], acol[:, :, near, :], edge[:, :, :, e], SUB))
                link(V.tensor_reduce(wsum[:, :, :, 3], acol[:], X, A))
                for e, row_out in ((2, 0), (1, 1), (0, 2), (4, H - 1), (5, H - 2), (6, H - 3)):
                    near = e + 1 if e < 3 else e - 1
                    link(T(wsum[:, :, :, e], wsum[:, :, :, near], acol[:, :, :, row_out], SUB))
                dve.wait_ge(s_l1p, 4 * b + 1)
                link(V.tensor_copy(cols(6, 2), tiny[:, 0:4].rearrange("p (t v) -> p t v", v=2)[:, :, 0]))
                link(T(cols(8, 2), cols(6, 2), cols(6, 2), M))
                link(T(cols(10, 2), tiny[:, 0:4].rearrange("p (t v) -> p t v", v=2)[:, :, 1], cols(8, 2), SUB))
                hops["var"] = link.count
                mean, std, r, nr = cols(6, 2), cols(12, 2), cols(14, 2), cols(22, 2)
                dve.wait_ge(s_l1a, 4 * b + 1)
                link(V.reciprocal(r, std))
                link(V.tensor_scalar(nr, r, -1.0 / N, None, M))
                flat = wsum[:].rearrange("p t d e -> p t (d e)")
                for t in range(CT):
                    link(S(flat[:, t, :], cnt, mean[:, t:t + 1], flat[:, t, :], M, SUB))
                    link(T(tmpw[:, t], w7s[:, t], flat[:, t:t + 1, :].broadcast_to([P, 3, 49]), M))
                mk = cols(16, 6).rearrange("p (t k) -> p t k", k=3)
                link(V.tensor_reduce(mk, tmpw[:], X, A))
                mean_k = cols(24, 6).rearrange("p (t k) -> p t k", k=3)
                bias_k = col[:, DWB:DWB + 6].rearrange("p (t k) -> p t k", k=3)
                for t in range(CT):
                    link(S(mean_k[:, t, :], mk[:, t, :], nr[:, t:t + 1], bias_k[:, t, :], M, A))
                hops["mean_k"] = link.count
                dve.wait_ge(s_l1p, 4 * b + 2)
                link(T(cols(30, 2), tiny[:, 8:10], col[:, BPW:BPW + 2], A))
                hops["g"] = link.count
                dve.wait_ge(s_l1p, 4 * b + 3)

                def hid(a):
                    return l1[0:64, a:a + 1]
                link(T(hid(32), tiny[0:64, 16:17], col[0:64, BA1:BA1 + 1], A))
                link(V.tensor_scalar(hid(33), hid(32), 20.0, None, ALU.min))
                hops["hid"] = link.count
                dve.wait_ge(s_l1a, 4 * b + 2)
                link(S(hid(35), hid(34), 2.0, hid(34), A, M))
                link(V.tensor_scalar(hid(36), hid(35), 2.0, None, A))
                link(V.reciprocal(hid(37), hid(36)))
                link(T(hid(38), hid(35), hid(37), M))
                link(T(hid(39), hid(38), hid(32), M))
                link(V.tensor_scalar(hbc[:], ones[0:64, :], hid(39), None, M))
                hops["hbc"] = link.count
                dve.wait_ge(s_l1p, 4 * b + 4)
                link(T(cols(40, 3), tiny[:, 24:27], ba2r, A))
                link(V.tensor_reduce(cols(43), cols(40, 3), X, ALU.max, negate=True))
                hops["logits"] = link.count
                dve.wait_ge(s_l1a, 4 * b + 3)
                link(V.tensor_reduce(cols(47), cols(44, 3), X, A))
                link(V.reciprocal(cols(48), cols(47)))
                link(V.tensor_scalar(cols(49, 3), cols(44, 3), cols(48), None, M))
                link(V.tensor_scalar(wk[:], w7s[:, :, 0, :], cols(49), None, M))
                for k in (1, 2):
                    link(S(wk[:], w7s[:, :, k, :], cols(49 + k), wk[:], M, A))
                link(T(wk[:, :, 24], wk[:, :, 24], std, A))
                weighted = cols(56, 6).rearrange("p (t k) -> p t k", k=3)
                link(T(weighted, bias_k, cols(49, 3).unsqueeze(1).broadcast_to([P, CT, 3]), M))
                link(V.tensor_reduce(cols(62, 2), weighted, X, A))
                dve.wait_ge(s_usto, 16 * 5 * b)
                link(T(svec[:, :, 3], cols(62, 2), mean, A))
                link(V.tensor_copy(svec[:, :, 0], mean))
                link(V.tensor_scalar(svec[:, :, 1], r, XS, None, M))
                link(V.tensor_reduce(cols(52, 2), wk[:], X, ALU.max, apply_absolute_value=True))
                link(V.reciprocal(cols(54, 2), cols(52, 2)))
                link(V.tensor_scalar(svec[:, :, 2], cols(52, 2), 1.0 / (KW * XS), None, M))
                for t in range(CT):
                    link(V.tensor_scalar(wk[:, t, :], wk[:, t, :], cols(54 + t), KW, M, M))
                hops["wk"] = link.count
                dve.wait_ge(s_l1a, 4 * b + 4)
                uk = uker[:, :, 0:SEG * 16].rearrange("p t (q j) -> p t q j", j=16)[:, :, :, 9:16]
                for t in range(CT):
                    link(T(uk[:, t, TAPS:SEG], wk[:, t, :].rearrange("p (d e) -> p d e", e=7),
                           uk[:, t, 0:TAPS], SUB))
                part(dve)
                assert link.count == N_L1, link.count

            def convolution(b, with_max):
                dve.wait_ge(s_uld, 16 * U_LOADS * (b + 1))
                V.tensor_tensor(mrow[:], sin[:, :, 1:2].broadcast_to([P, NG, NT]),
                                cst[:, 0:NT].unsqueeze(1).broadcast_to([P, NG, NT]), ALU.mult).then_inc(s_mr, 1)
                dve.wait_ge(s_mr, b + 1)
                part(dve)

                def prepare(gi, u, loads):
                    n = b * NG + gi
                    dve.wait_ge(s_xw[u], 16 * (b * (NG // 2) + loads))
                    dve.wait_ge(s_xgh, n)
                    dve.wait_ge(s_xgl, n)
                    V.scalar_tensor_tensor(xg[:], xw[:, u], sin[:, gi, 0:1],
                                           mrow[:, gi, :].unsqueeze(2).broadcast_to([P, NT, W]),
                                           ALU.subtract, ALU.mult).then_inc(s_xg, 1)
                    dve.wait_ge(s_cv, n + 1)
                    V.tensor_tensor(tmat[:, u], vker[:, gi, :, 0:TO].unsqueeze(3).broadcast_to([P, SEG, TO, GC]),
                                    maskc[:].unsqueeze(1).unsqueeze(1).broadcast_to([P, SEG, TO, GC]),
                                    ALU.mult).then_inc(s_tm, 1)
                    dve.wait_ge(s_xgh, n + 1)
                    V.tensor_tensor(xgl[:, u], xg[:], xgh[:, u], ALU.subtract).then_inc(s_xgl, 1)

                mxs = mx[:].rearrange("p n c -> p (n c)")

                def maxima(gi, u):
                    if with_max:
                        max_step((b + 1) * NCH * MAXSTEPS + gi, mxs[:, ds(gi, 1)], u)

                prepare(0, 0, 1)
                with dve.Fori(0, NG // 2 - 1) as h:
                    prepare(h * 2 + 1, 1, h + 1)
                    maxima(h * 2, 0)
                    prepare(h * 2 + 2, 0, h + 2)
                    maxima(h * 2 + 1, 1)
                prepare(NG - 1, 1, NG // 2)
                maxima(NG - 2, 0)
                maxima(NG - 1, 1)

            first_image(dve, first_chunk)
            feature_chunk(0, NCH - 1)
            dve.wait_ge(s_xfree, 2 + B * NCH)
            image_statistics(1, B)
            max_pass(0)
            dve.wait_ge(s_setp, 4)
            image_scalars(1, B, 2)
            dve.wait_ge(s_lload, 16 * 4)
            with dve.Fori(0, B - 1) as b:
                attention(b, True)
                layer1(b)
                features(b + 1)
                convolution(b, True)
            attention(B - 1, False)
            layer1(B - 1)
            convolution(B - 1, False)

        @block.scalar
        def _(act):
            A = nc.scalar.activation

            def feature_chunk(b, j):
                cs = ts(j, CHUNK)
                act.wait_ge(s_qkps, b * NCH + j + 1)
                act.wait_ge(s_qk, b * NCH + j)
                A(qk32[:], bank[0][0:64, :], ACT.Identity, bias=qk_bias[:], scale=qk_scale[:]).then_inc(s_qk32, 1)
                act.wait_ge(s_qk32, b * NCH + j + 1)
                A(bq[0:32, cs], qk32[0:32], ACT.Copy)
                A(bq[64:96, cs], qk32[0:32], ACT.Copy)
                A(ck[0:32, cs], qk32[32:64], ACT.Copy)
                A(ck[32:64, cs], qk32[32:64], ACT.Copy).then_inc(s_qkh, 1)
                for u in range(4):
                    act.wait_ge(s_vps, b * KEYT + j * 4 + u + 1)
                    A(vh[:, j * 4 + u, 0:C], bank[1 + u][:, 0:C], ACT.Copy, scale=DV_SHIFT).then_inc(s_vhi, 1)

            def features(b):
                with act.Fori(0, NCH) as j:
                    feature_chunk(b, j)

            def normalise(pair, odd, first, last):
                act.wait_ge(s_hx[odd], 16 * CT * (pair + 1))
                for t in range(CT):
                    rowsx = hxs[odd][:, t, 0:ROWS + 2 - first - last, :]
                    A(rowsx, rowsx, ACT.Identity, bias=gnp[:, 0, t, 1:2], scale=gnp[:, 0, t, 0:1]).then_inc(s_norm, 1)

            def first_chunk(pair, odd, first, last):
                q = pair * 2 + odd
                if first:
                    normalise(0, 0, 1, 0)
                if not last:
                    normalise(pair + odd, 1 - odd, 0, 0)
                if not first:
                    feature_chunk(0, q - 1)
                act.wait_ge(s_maxp, q + 1)
                A(cath[:, CT:KT, ts(q, CHUNK)], pooled[1][:], ACT.Copy).then_inc(s_high, 1)
                act.wait_ge(s_pool, N_SUM0 * (q + 1) + 1 + last)
                A(cath[:, 0:CT, ts(q, CHUNK)], pooled[0][:], ACT.Copy).then_inc(s_high, 1)

            def exp_step(s, i):
                act.wait_ge(s_st, s + 1)
                act.wait_ge(s_pv, s + 1)
                A(ph[i], sT[i % 2][:], ACT.Exp, bias=lnp[:], scale=escale[:])
                A(p32[i], sT[i % 2][:], ACT.Exp, bias=lnp[:], scale=escale[:]).then_inc(s_exp, 1)

            def store_rows(r, g):
                act.wait_ge(s_mrow, r + 1)
                A(bq[96:98, ts(g, CHUNK)], aux[0][96:98, :], ACT.Copy).then_inc(s_rows, 1)

            def group(b, g, with_next):
                r = b * NCH + g
                s0 = r * KEYT
                with act.Fori(0, 7) as i:
                    for u in range(4):
                        exp_step(s0 + i * 4 + u + 2, (u + 2) % 4)
                for u in range(2):
                    exp_step(s0 + 28 + u + 2, (u + 2) % 4)
                if with_next:
                    store_rows(r + 1, g + 1)
                    for u in range(2):
                        exp_step(s0 + KEYT + u, u)
                act.wait_ge(s_turn, CT * r)
                for nb in range(NB):
                    act.wait_ge(s_rden, NB * r + nb + 1)
                    A(onorm[:, nb, :], acc[nb][:, 0:C], ACT.Copy, scale=rden[:, nb:nb + 1]).then_inc(s_on, 1)

            def attention(b):
                store_rows(b * NCH, 0)
                for u in range(2):
                    exp_step(b * NCH * KEYT + u, u)
                with act.Fori(0, NCH - 1) as g:
                    group(b, g, True)
                group(b, NCH - 1, False)

            def layer1(b):
                c0 = b * N_L1
                act.wait_ge(s_l1, c0 + hops["var"])
                A(l1[:, 12:14], l1[:, 10:12], ACT.Sqrt, bias=epst[:]).then_inc(s_l1a, 1)
                act.wait_ge(s_l1, c0 + hops["hid"])
                A(l1[0:64, 34:35], l1[0:64, 33:34], ACT.Exp).then_inc(s_l1a, 1)
                act.wait_ge(s_l1, c0 + hops["logits"])
                A(l1[:, 44:47], l1[:, 40:43], ACT.Exp, bias=l1[:, 43:44]).then_inc(s_l1a, 1)
                act.wait_ge(s_l1, c0 + hops["wk"])
                uk = uker[:, :, 0:SEG * 16].rearrange("p t (q j) -> p t q j", j=16)[:, :, :, 9:16]
                for t in range(CT):
                    ins = A(uk[:, t, 0:TAPS], wk[:, t, :].rearrange("p (d e) -> p d e", e=7), ACT.Copy)
                ins.then_inc(s_l1a, 1)

            def high_part(b, gi, u):
                n = b * NG + gi
                act.wait_ge(s_xg, n + 1)
                act.wait_ge(s_cv, n + 1)
                A(xgh[:, u], xg[:], ACT.Copy).then_inc(s_xgh, 1)

            def evacuate(b, gi, h, u):
                n = b * NG + gi
                act.wait_ge(s_cv, 2 + n + 1)
                act.wait_ge(s_out[u], 16 * SP_STORES * (b * (NG // 2) + h))
                act.wait_ge(s_outp[u], 16 * POOL_STORES * (b * (NG // 2) + h))
                A(yo[:, u], acc[u][0:MO, 0:NT * W].rearrange("p (t w) -> p t w", w=W), ACT.Identity,
                  bias=sout[:, gi, 1:2], scale=sout[:, gi, 0:1]).then_inc(s_y, 1)

            def convolution(b):
                act.wait_ge(s_uld, 16 * U_LOADS * (b + 1))
                for u in range(2):
                    high_part(b, u, u)
                with act.Fori(0, NG // 2 - 1) as h:
                    for u in range(2):
                        evacuate(b, h * 2 + u, h, u)
                        high_part(b, h * 2 + u + 2, u)
                for u in range(2):
                    evacuate(b, NG - 2 + u, NG // 2 - 1, u)

            def deviations(b0, b1):
                act.wait_ge(s_set, hops["var0", b0])
                some = slice(b0 * CT, b1 * CT)
                A(gn0[:, 4, some], gn0[:, 3, some], ACT.Sqrt, bias=epst[:]).then_inc(s_seta, 1)

            deviations(0, 1)
            act.wait_ge(s_set, hops["gnp", 0])
            first_image(act, first_chunk)
            feature_chunk(0, NCH - 1)
            deviations(1, B)
            act.wait_ge(s_zero, 16 * 4 * B)
            with act.Fori(0, B - 1) as b:
                attention(b)
                layer1(b)
                features(b + 1)
                convolution(b)
            attention(B - 1)
            layer1(B - 1)
            convolution(B - 1)

        @block.tensor
        def _(pe):
            MM = nc.tensor.matmul
            NW = C + 2 * C8

            def product3(out_ap, stat, mov, start, stop):
                terms = [(s, m) for sh, sl, mh, ml in zip(*stat, *mov) for s, m in ((sh, mh), (sh, ml), (sl, mh))]
                for i, (s, m) in enumerate(terms):
                    ins = MM(out_ap, s, m, start=start and i == 0, stop=stop and i == len(terms) - 1)
                return ins

            def features(b, first=False):
                pe.wait_ge(s_on, NB * NCH * b)
                pe.wait_ge(s_exp, NCH * KEYT * b)
                part(pe)
                with pe.Fori(0, NCH) as j:
                    cs = ts(j, CHUNK)
                    pe.wait_ge(s_cat, b * NCH + j + 1)
                    if first:
                        pe.wait_ge(s_maxlow, j + 1)
                    pe.wait_ge(s_qk32, b * NCH + j)
                    ks = range(KT)
                    product3(bank[0][0:64, :], ([wh[:, k, C:NW] for k in ks], [wl[:, k, C:NW] for k in ks]),
                             ([cath[:, k, cs] for k in ks], [catl[:, k, cs] for k in ks]), True, True)\
                        .then_inc(s_qkps, 1)
                    for u in range(4):
                        pe.wait_ge(s_vlo, b * KEYT + j * 4 + u + 1)
                        tc = ts(j * 4 + u, P)
                        product3(bank[1 + u][:, 0:C], ([cath[:, k, tc] for k in ks], [catl[:, k, tc] for k in ks]),
                                 ([wh[:, k, 0:C] for k in ks], [wl[:, k, 0:C] for k in ks]), True, True)\
                            .then_inc(s_vps, 1)

            def max_block(n, q, k, e):
                pe.wait_ge(s_mfree, n + 1)
                MM(aux[e][:], bq[0:96, q], ck[0:96, k], start=True, stop=True).then_inc(s_mps, 1)

            def max_pass(b):
                with pe.Fori(0, NB) as nb:
                    for c in range(NCH):
                        max_block(b * NCH * MAXSTEPS + nb * NCH + c, ts(nb, P), ts(c, CHUNK), c % 2)

            def turn_maxima(r):
                pe.wait_ge(s_m2, r + 1)
                for nb in range(NB):
                    ins = MM(aux[0][96:98, nb * P:(nb + 1) * P], m2[:, nb, :], identh[:], start=True, stop=True)
                ins.then_inc(s_mrow, 1)

            def scores(g, t, i):
                MM(sT[i % 2][:], ck[0:98, ts(t, P)], bq[0:98, ts(g, CHUNK)], start=True, stop=True).then_inc(s_st, 1)

            def group(b, g, with_finish, with_next, first_group):
                r = b * NCH + g
                s0 = r * KEYT

                def step(i, u, first, last, maxima):
                    s = s0 + i * 4 + u
                    if not last or u < 2:
                        pe.wait_ge(s_exp, s + 1)
                        scores(g, i * 4 + u + 2, u)
                    elif with_next:
                        pe.wait_ge(s_exp, s + 1)
                        if u == 2:
                            pe.wait_ge(s_rows, r + 2)
                        scores(g + 1, u - 2, u)
                    pe.wait_ge(s_lo, s + 1)
                    start, stop = first and u == 0, last and u == 3
                    t = i * 4 + u
                    for nb in range(NB):
                        if maxima and nb % 2 == 0:
                            e = nb // 2
                            max_block((r + 1) * MAXSTEPS + i * 8 + 2 * u + e, ds((g + 1) * CHUNK + i * P, P),
                                      ts(2 * u + e, CHUNK), e)
                        if start and not first_group:
                            pe.wait_ge(s_on, NB * (r - 1) + nb + 1)
                        q = slice(nb * P, (nb + 1) * P)
                        MM(acc[nb][:, 0:C + 1], ph[u][:, q], vh[:, t, 0:C + 1], start=start, stop=False)
                        MM(acc[nb][:, 0:C], ph[u][:, q], vl[:, t, :], start=False, stop=False)
                        ins = MM(acc[nb][:, 0:C + 1], pl[u][:, q], vh[:, t, 0:C + 1], start=False, stop=stop)
                        if stop and nb < NB - 1:
                            ins.then_inc(s_acc, 1)
                    ins.then_inc(s_pv, 1)

                for u in range(4):
                    step(0, u, True, False, with_next)
                with pe.Fori(1, 4) as i:
                    for u in range(4):
                        step(i, u, False, False, with_next)
                if with_finish:
                    turn_sums(r - 1, (r + 2) if with_next else (r + 1))
                with pe.Fori(4, 7) as i:
                    for u in range(4):
                        step(i, u, False, False, False)
                if with_next:
                    if with_finish:
                        pe.wait_ge(s_x1, CT * r)
                    else:
                        pe.wait_ge(s_mfree, 2 + MAXSTEPS * (r + 2))
                    turn_maxima(r + 1)
                for u in range(4):
                    step(7, u, False, True, False)

            def turn_sums(r, groups):
                pe.wait_ge(s_on, NB * (r + 1))
                pe.wait_ge(s_mfree, 2 + MAXSTEPS * groups)
                for t in range(CT):
                    for nb in range(NB):
                        ins = nc.tensor.transpose(aux[t][:, nb * P:(nb + 1) * P], onorm[:, nb, t * P:(t + 1) * P],
                                                  ident)
                    ins.then_inc(s_turn, 1)

            def attention(b):
                pe.wait_ge(s_mfree, 2 + MAXSTEPS * (b * NCH + 1))
                turn_maxima(b * NCH)
                pe.wait_ge(s_vlo, 4 + KEYT * (b + 1))
                pe.wait_ge(s_y, 2 + NG * b)
                pe.wait_ge(s_rows, b * NCH + 1)
                for u in range(2):
                    scores(0, u, u)
                group(b, 0, False, True, True)
                with pe.Fori(1, NCH - 1) as g:
                    group(b, g, True, True, False)
                group(b, NCH - 1, True, False, False)
                turn_sums(b * NCH + NCH - 1, b * NCH + NCH)

            def layer1(b):
                c0 = b * N_L1
                pe.wait_ge(s_exp, NCH * KEYT * (b + 1))
                pe.wait_ge(s_l1, c0 + hops["me"])
                MM(tiny[:, 0:4], gmat, l1[:, 0:4], start=True, stop=True).then_inc(s_l1p, 1)
                pe.wait_ge(s_l1, c0 + hops["mean_k"])
                for o in range(CT):
                    for i in range(3 * CT):
                        k, t = i // CT, i % CT
                        ins = MM(tiny[:, 8 + o:9 + o], wpws[:, i, o * P:(o + 1) * P],
                                 l1[:, 24 + t * 3 + k:25 + t * 3 + k], start=(i == 0), stop=(i == 3 * CT - 1))
                ins.then_inc(s_l1p, 1)
                pe.wait_ge(s_l1, c0 + hops["g"])
                for o in range(CT):
                    ins = MM(tiny[0:64, 16:17], wa1s[:, o, :], l1[:, 30 + o:31 + o], start=(o == 0), stop=(o == CT - 1))
                ins.then_inc(s_l1p, 1)
                pe.wait_ge(s_l1, c0 + hops["hbc"])
                MM(tiny[:, 24:27], hbc[:], wa2s[:], start=True, stop=True).then_inc(s_l1p, 1)

            def convolve(b, gi, u):
                n = b * NG + gi
                pe.wait_ge(s_y, n + 1)
                pe.wait_ge(s_xgh, n + 1)
                pe.wait_ge(s_tm, n + 1)
                pe.wait_ge(s_xgl, n + 1)
                out3 = acc[u][0:MO, 0:NT * W].rearrange("p (t w) -> p t w", w=W)
                order = [3, 2, 4, 1, 5, 0, 6]
                for d in order:
                    lo, hi = max(0, 3 - d), W - max(0, d - 3)
                    for i, (q, xp) in enumerate(((d, xgh), (d, xgl), (TAPS + d, xgh))):
                        ins = MM(out3[:, :, lo:hi], tmat[:, u, q].rearrange("p m c -> p (m c)"),
                                 xp[:, u, :, lo + d - 3:hi + d - 3],
                                 start=(d == 3 and i == 0), stop=(d == 6 and i == 2))
                ins.then_inc(s_cv, 1)

            def convolution(b, with_max):
                if with_max:
                    pe.wait_ge(s_qk, NCH * (b + 2))
                    pe.wait_ge(s_x1, CT * NCH * (b + 1))
                pe.wait_ge(s_vlo, 4 + KEYT * (b + 1 + with_max))
                part(pe)
                with pe.Fori(0, NB) as nb, pe.Fori(0, NCH // 2) as h:
                    for u in range(2):
                        gi = nb * NCH + h * 2 + u
                        if with_max:
                            max_block((b + 1) * NCH * MAXSTEPS + gi, ts(nb, P), ts(h * 2 + u, CHUNK), u)
                        convolve(b, gi, u)

            def group_means(b0, b1):
                pe.wait_ge(s_set, hops["me0", b0])
                MM(tiny[:, 2 * b0 * CT:2 * b1 * CT], gmat, me0[:, b0 * CT:b1 * CT].rearrange("p i v -> p (i v)"),
                   start=True, stop=True).then_inc(s_setp, 1)

            group_means(0, 1)
            pe.wait_ge(s_set, hops["wabs"])
            for k in range(KT):
                ins = MM(bank[0][:, 0:NW], ones[:], wabs[:, k, :], start=(k == 0), stop=(k == KT - 1))
            ins.then_inc(s_setp, 1)
            pe.wait_ge(s_set, hops["wtot"])
            for t in range(CT):
                ins = MM(bank[1][:, t:t + 1], wtot[0:1, t * P:(t + 1) * P], ones[0:1, 0:1], start=True, stop=True)
            ins.then_inc(s_setp, 1)
            pe.wait_ge(s_set, hops["vdesc"])
            features(0, True)
            group_means(1, B)
            pe.wait_ge(s_qk, NCH)
            max_pass(0)
            with pe.Fori(0, B - 1) as b:
                attention(b)
                layer1(b)
                features(b + 1)
                convolution(b, True)
            attention(B - 1)
            layer1(B - 1)
            convolution(B - 1, False)

        @block.gpsimd
        def _(pool):
            G = nc.gpsimd

            def pools(b, q, first, last):
                n = b * NCH + q
                nrow = ROWS + 2 - first - last
                pool.wait_ge(s_hx[0], 16 * CT * (n + 1 - NCH // 2))
                part(pool)
                for t in range(CT):
                    rowsx = hx[:, t, 0:nrow, :]
                    G.tensor_scalar(rowsx, rowsx, gcur[:, t, 0:1], gcur[:, t, 1:2], ALU.mult, ALU.add)\
                        .then_inc(s_norm, 1)
                pool.wait_ge(s_norm, CT * (n + 1))
                part(pool)
                link = chain(pool, s_pool, NCH * N_SUM0 + (n - NCH) * N_SUM + 2 * b + (0 if first else 1),
                             parted=True)
                windows(link, G, ALU.add, 0, first, last)

                def split(kind):
                    dst_h, dst_l = (c[:, kind * CT:(kind + 1) * CT, ts(q, CHUNK)] for c in (cath, catl))
                    link(G.tensor_copy(dst_h, pooled[kind][:]))
                    return G.tensor_tensor(dst_l, pooled[kind][:], dst_h, ALU.subtract)
                link(split(0))
                pool.wait_ge(s_maxp, n + 1)
                part(pool)
                split(1).then_inc(s_cat, 1)
                pool.wait_ge(s_cat, n + 1)
                part(pool)
                assert link.count == N_SUM + first + last, link.count

            def image(b):
                G.tensor_copy(gcur[:], gnp[:, b, :, 0:2]).then_inc(s_gcur, 1)
                pool.wait_ge(s_gcur, b)
                part(pool)
                pools(b, 0, 1, 0)
                with pool.Fori(1, NCH - 1) as q:
                    pools(b, q, 0, 0)
                pools(b, NCH - 1, 0, 1)

            G.memset(threes[0][:], 0.0).then_inc(s_poolset, 1)
            pool.wait_ge(s_poolset, 1)

            def first_chunk(pair, odd, first, last):
                q = pair * 2 + odd
                pool.wait_ge(s_norm, CT * (q + 1))
                part(pool)
                windows(chain(pool, s_pool, q * N_SUM0 + 1 - first, parted=True), G, ALU.add, 0, first, last,
                        hxs[odd])
                pool.wait_ge(s_high, 2 * q + 2)
                part(pool)
                G.tensor_tensor(catl[:, 0:CT, ts(q, CHUNK)], pooled[0][:], cath[:, 0:CT, ts(q, CHUNK)],
                                ALU.subtract).then_inc(s_cat, 1)
                pool.wait_ge(s_cat, q + 1)
                part(pool)

            first_image(pool, first_chunk)
            pool.wait_ge(s_set, hops["gnp", 1])
            def stores_of(b):
                with pool.Fori(0, NG // 2) as h:
                    for u in range(2):
                        store_y(pool, b, h * 2 + u, u, range(SP_STORES, Y_STORES), s_outp)

            with pool.Fori(1, B) as b:
                pool.wait_ge(s_vps, b * KEYT)
                part(pool)
                image(b)
                stores_of(b - 1)
            stores_of(B - 1)

        @block.sync
        def _(sp):
            with sp.Fori(0, NCH // 2) as h:
                for u in range(2):
                    sp.wait_ge(s_xfree, h * 2 + u + 1)
                    sp.dma_start(xin[:, u], xv[0, :, :, ts(h * 2 + u, CHUNK)]).then_inc(s_xin[u], 16)
            sp.dma_start(cst_all[:], consts).then_inc(s_load, 16)
            for dst, src in ((col[:], cols), (row[:], rows)):
                sp.dma_start(dst, src).then_inc(s_load, 16)

            def halo_rows(b, q, hx, s_loaded):
                r0 = max(0, ROWS * q - 1) if isinstance(q, int) else ROWS * q - 1
                n = ROWS + 1 if isinstance(q, int) and q in (0, NCH - 1) else ROWS + 2
                for t in range(CT):
                    sp.dma_start(hx[:, t, 0:n, :].rearrange("p r w -> p (r w)"),
                                 xv[b, :, t, ds(r0 * W, n * W)]).then_inc(s_loaded, 16)

            halo_rows(0, 0, hxs[0], s_hx[0])
            halo_rows(0, 1, hxs[1], s_hx[1])
            sp.dma_start(wraw, wall).then_inc(s_wload, 16)

            def first_chunk(pair, odd):
                q = pair * 2 + odd
                for image in range(1, B):
                    u, _, chunks = stat_chunk(pair, odd, image)
                    sp.wait_ge(s_xfree, chunks)
                    sp.dma_start(xin[:, u], xv[image, :, :, ts(q, CHUNK)]).then_inc(s_xin[u], 16)
                sp.wait_ge(s_cat, q + 1)
                sp.wait_ge(s_maxp, q + 1)
                if isinstance(q, int) and q + 2 >= NCH:
                    return
                halo_rows(0, q + 2, hxs[odd], s_hx[odd])

            with sp.Fori(0, NCH // 2 - 2) as h:
                first_chunk(h, 0)
                first_chunk(h, 1)
            for q in range(NCH - 4, NCH):
                first_chunk(q // 2, q % 2)
            for dst, src in ((w7s[:], w7), (wpws[:], wpw), (wa1s[:], wa1), (wa2s[:], wa2)):
                sp.dma_start(dst, src).then_inc(s_lload, 16)

            low = H + 3 - (NT - 1) * TO
            with sp.Fori(0, B) as b:
                for t in range(CT):
                    for win, a, z in ((0, 0, 3), (NT - 1, low, WIN)):
                        sp.dma_start(bass.AP(x1w, b * (NT * C * WIN * W) + (t * P * WIN * NT + a * NT + win) * W,
                                             [[WIN * NT * W, P], [NT * W, z - a], [1, W]]),
                                     zeros[:, 0:(z - a) * W]).then_inc(s_zero, 16)

            def halo_load(b, q):
                sp.wait_ge(s_cat, b * NCH + q)
                halo_rows(b, q, hx, s_hx[0])

            def store_x1(b, g):
                sp.wait_ge(s_x1, (b * NCH + g + 1) * CT)
                for t, a, z in pieces[g]:
                    k = a + 3 - TO * t
                    for ct in range(CT):
                        sp.dma_start(bass.AP(x1w, b * (NT * C * WIN * W) + (ct * P * WIN * NT + k * NT + t) * W,
                                             [[WIN * NT * W, P], [NT * W, z - a], [1, W]]),
                                     x1c[:, ct, (a - ROWS * g) * W:(z - ROWS * g) * W]).then_inc(s_x1o, 16)
                sp.wait_ge(s_x1o, 16 * (stores[NCH] * b + stores[g + 1]))
                part(sp)

            def attention(b, pool_next):
                for g in range(NCH):
                    if pool_next:
                        halo_load(b + 1, g)
                    if g:
                        store_x1(b, g - 1)
                    sp.dma_start(xin[:, 0], xv[b, :, :, ts(g, CHUNK)]).then_inc(s_xr, 16)
                store_x1(b, NCH - 1)

            def layer1(b):
                sp.wait_ge(s_l1, N_L1 * (b + 1))
                part(sp)
                sp.wait_ge(s_uld, 16 * U_LOADS * b)
                sp.dma_start(bass.AP(kern, 0, [[ULEN, P], [P * ULEN, CT], [1, ULEN]]), uker[:])\
                    .then_inc(s_usto, 16)
                for dst, v in ((scal_in, 0), (scal_out, 2)):
                    for t in range(CT):
                        sp.dma_start(bass.AP(dst, b * (GC * NG * 2) + t * (NG // CT) * 2,
                                             [[2, NG // CT], [NG * 2, GC], [1, 2]]),
                                     svec[:, t, v:v + 2]).then_inc(s_usto, 16)
                sp.wait_ge(s_usto, 16 * 5 * (b + 1))
                for k in range(WIN):
                    sp.dma_start(vker[k::WIN].rearrange("c g q j -> c g (q j)"),
                                 bass.AP(kern, WIN - 1 - k, [[ULEN, GC], [GC * ULEN, NG], [1, SEG * 16]]))\
                        .then_inc(s_uld, 16)
                sp.dma_start(sin[:].rearrange("p g v -> p (g v)"),
                             bass.AP(scal_in, b * (GC * NG * 2), [[NG * 2, GC], [0, WIN], [1, NG * 2]]))\
                    .then_inc(s_uld, 16)
                sp.dma_start(sout[:].rearrange("p g v -> p (g v)"),
                             bass.AP(scal_out, b * (GC * NG * 2), [[0, TO], [NG * 2, GC], [1, NG * 2]]))\
                    .then_inc(s_uld, 16)

            def window_load(b, gi, u):
                sp.dma_start(xw[:, u], bass.AP(x1w, b * (NT * C * WIN * W) + gi * (GC * WIN * NT * W),
                                               [[NT * W, P], [W, NT], [1, W]])).then_inc(s_xw[u], 16)

            def convolution(b):
                def next_load(gi, u):
                    sp.wait_ge(s_xg, b * NG + gi + 1)
                    window_load(b, gi + 2, u)
                for u in range(2):
                    window_load(b, u, u)
                next_load(0, 0)
                with sp.Fori(0, NG // 2 - 2) as h:
                    for u in range(2):
                        next_load(h * 2 + u + 1, 1 - u)
                        store_y(sp, b, h * 2 + u, u, range(SP_STORES), s_out)
                next_load(NG - 3, 1)
                for gi in range(NG - 4, NG):
                    store_y(sp, b, gi, gi % 2, range(SP_STORES), s_out)

            sp.wait_ge(s_zero, 16 * 4 * B)
            sp.wait_ge(s_xfree, 2 + B * NCH)
            with sp.Fori(0, B - 1) as b:
                attention(b, True)
                layer1(b)
                convolution(b)
            attention(B - 1, False)
            layer1(B - 1)
            convolution(B - 1)
            for u in range(2):
                sp.wait_ge(s_out[u], 16 * SP_STORES * B * NG // 2)
                sp.wait_ge(s_outp[u], 16 * POOL_STORES * B * NG // 2)


def kernel(**inputs):
    import concourse.bacc as bacc
    from concourse.bass_utils import run_bass_kernel_spmd

    a = {k: np.asarray(v) for k, v in inputs.items()}

    def tiles(w):
        return np.ascontiguousarray(w.reshape(-1, P, w.shape[-1]).transpose(1, 0, 2))

    def vec(v):
        v = v.reshape(-1)
        if v.size < P:
            return np.pad(v, (0, P - v.size)).reshape(P, 1)
        return np.ascontiguousarray(v.reshape(-1, P).T)

    def kernel7(w):
        e = (TAPS - w.shape[-1]) // 2
        w = np.pad(w[:, 0], ((0, 0), (e, e), (e, e)))
        return np.ascontiguousarray(w.transpose(0, 2, 1)[:, :, ::-1]).reshape(C, 49)

    channel, shift = np.arange(P), np.abs(np.arange(7) - 3)
    groups = (channel[:, None] // GN_GROUP == channel[None] // GN_GROUP) / GN_GROUP
    at_row = TO * np.arange(NT)[None] + (channel % WIN)[:, None] - 3
    inside = (at_row >= 0) & (at_row < H)
    of_channel = channel[:, None] // WIN == np.arange(GC)[None]
    count = ((W - shift)[:, None] * (H - shift)[None]).reshape(1, 49)
    consts = np.concatenate([np.eye(P), groups, inside, of_channel], axis=1).astype(np.float32)

    w7 = np.stack([kernel7(a[f"L1_conv_w{k}"]) for k in (3, 5, 7)], axis=1)
    dwb = np.stack([vec(a[f"L1_conv_b{k}"]) for k in (3, 5, 7)], axis=2).reshape(P, 6)
    cols = np.concatenate([vec(a["L0_conv_bd"]), vec(a["L1_conv_b_pw"]), dwb,
                           vec(np.concatenate([a["L0_conv_bb"], a["L0_conv_bc"]])), vec(a["L1_conv_b_a1"])], axis=1)
    row = np.concatenate([a["L0_conv_bb"], a["L0_conv_bc"], a["L1_conv_b_a2"], a["L0_conv_alpha"].reshape(1),
                          count.astype(np.float32)[0]])
    arrays = {
        "x": a["x"].reshape(B, C, N),
        "wall": tiles(np.concatenate([a["L0_conv_wd"], a["L0_conv_wb"], a["L0_conv_wc"]]).T),
        "w7": tiles(w7.reshape(C, -1)).reshape(P, CT, 3, 49),
        "wpw": tiles(a["L1_conv_w_pw"].T),
        "wa1": tiles(a["L1_conv_w_a1"].T),
        "wa2": a["L1_conv_w_a2"].T,
        "cols": cols,
        "rows": np.broadcast_to(row, (P, row.size)),
        "consts": consts,
    }
    arrays = {k: np.ascontiguousarray(v) for k, v in arrays.items()}
    nc = bacc.Bacc("TRN2", target_bir_lowering=False, num_devices=1)
    aps = [nc.dram_tensor(k, v.shape, mybir.dt.from_np(v.dtype), kind="ExternalInput").ap()
           for k, v in arrays.items()]
    out = nc.dram_tensor("out", [B, C, N], F32, kind="ExternalOutput").ap()
    build(nc, *aps, out)
    r = run_bass_kernel_spmd(nc, [arrays], core_ids=[0])
    return r.results[0]["out"].reshape(B, C, H, W)
```

```python
from contextlib import ExitStack

import numpy as np

import concourse.bass as bass
from concourse import mybir

F32, F16 = mybir.dt.float32, mybir.dt.float16
ALU = mybir.AluOpType
ACT = mybir.ActivationFunctionType
X, XY = mybir.AxisListType.X, mybir.AxisListType.XY

B, C, H, W = 4, 256, 64, 64
N = H * W
P = 128
CT = C // P
C8 = C // 8
KT = 2 * CT
GN_GROUP = 8
CHUNK = 512
NCH = N // CHUNK
KEYT = N // P
NB = CHUNK // P
ROWS = CHUNK // W
GC, WIN, TO = 8, 16, 10
TAPS = 7
NT = -(-H // TO)
NG = C // GC
SEG = 2 * TAPS
ULEN = SEG * 16 + 16
MO = TO * GC
GN_MAX = 182.0
XS = 16.0
WS = 2048.0
MAXROW = 32768.0
QK_TOP = 4096.0
P_TOP = 512.0
DV_SHIFT = 2.0 ** -8
DV_SCALE = XS * WS * DV_SHIFT
KW = 256.0
EPS = 1e-5


def build(nc, x, wall, w7, wpw, wa1, wa2, cols, rows, consts, out):
    ctx = ExitStack()
    with ctx:
        def sb(name, shape, dt=F32):
            return ctx.enter_context(nc.sbuf_tensor(name, shape, dt))

        def sem(name):
            return ctx.enter_context(nc.semaphore(name))

        x1w = nc.dram_tensor("x1w", [B, C, WIN, NT, W], F32)
        kern = nc.dram_tensor("kern", [C, ULEN], F16)
        scal_in = nc.dram_tensor("scal_in", [B, GC, NG, 2], F32)
        scal_out = nc.dram_tensor("scal_out", [B, GC, NG, 2], F32)

        cst_all = sb("cst_all", [P, 2 * P + NT + GC])
        ident, gmat = cst_all[:, 0:P], cst_all[:, P:2 * P]
        cst = cst_all[:, 2 * P:]
        identh = sb("identh", [P, P], F16)
        maskc = sb("maskc", [P, GC], F16)
        ones = sb("ones", [P, P])
        wh = sb("wh", [P, KT, C], F16)
        wl = sb("wl", [P, KT, C], F16)
        wqk = sb("wqk", [P, KT, 4 * C8], F16)
        w7s = sb("w7s", [P, CT, 3, 49])
        wpws = sb("wpws", [P, 3 * CT, C])
        wa1s = sb("wa1s", [P, CT, 64])
        wa2s = sb("wa2s", [64, 3])
        col = sb("col", [P, 12])
        row = sb("row", [P, 64 + 3 + 1 + 49])
        BD, BPW, DWB, BBC, BA1 = 0, 2, 4, 10, 11
        bbrow, ba2r, alpha, cnt = row[:, 0:64], row[:, 64:67], row[:, 67:68], row[:, 68:117]

        small = sb("small", [P, 16])
        escale = sb("escale", [P, 1])
        lnp = sb("lnp", [P, 1])
        epst = sb("epst", [P, 1])
        qk_scale = sb("qk_scale", [P, 1])
        qk_bias = sb("qk_bias", [64, 1])
        vdesc = sb("vdesc", [P, CT])
        xin = sb("xin", [P, 2, CT, CHUNK])
        st0 = sb("st0", [P, B, NCH, CT, 6])
        me0 = sb("me0", [P, B * CT, 2])
        gn0 = sb("gn0", [P, 8, B * CT])
        gnp = sb("gnp", [P, B, CT, 4])

        hx = sb("hx", [P, CT, ROWS + 2, W])
        gcur = sb("gcur", [P, CT, 2])
        pairs = [sb(f"pairs_{o}", [P, CT, (ROWS + 1) * W]) for o in ("sum", "max")]
        threes = [sb(f"threes_{o}", [P, CT, ROWS, W + 2]) for o in ("sum", "max")]
        pooled = [sb(f"pooled_{o}", [P, CT, CHUNK]) for o in ("sum", "max")]
        cath = sb("cath", [P, KT, N], F16)
        catl = sb("catl", [P, KT, N], F16)
        x0 = cath[:].rearrange("p k n -> p (k n)").bitcast(F32).rearrange("p (h t n) -> p h t n", h=NCH // 2, t=CT)

        vh = sb("vh", [P, KEYT, C + 2], F16)
        vl = sb("vl", [P, KEYT, C], F16)
        bq = sb("bq", [P, N], F16)
        ck = sb("ck", [P, N], F16)
        qk32 = sb("qk32", [64, CHUNK])
        pbuf = sb("pbuf", [P, 4, 2 * CHUNK])
        p32 = [pbuf[:, i, 0:CHUNK] for i in range(4)]
        ph = [pbuf[:, i, CHUNK:CHUNK + 256].bitcast(F16) for i in range(4)]
        pl = [pbuf[:, i, CHUNK + 256:2 * CHUNK].bitcast(F16) for i in range(4)]
        flatp = pbuf[:].rearrange("p a b -> p (a b)")
        NW = C + 2 * C8
        wraw = flatp[:, 0:KT * NW].rearrange("p (k n) -> p k n", k=KT)
        wabs = flatp[:, KT * NW:2 * KT * NW].rearrange("p (k n) -> p k n", k=KT)
        wtot = flatp[:, 2 * KT * NW:(2 * KT + 1) * NW]
        wscale = flatp[:, (2 * KT + 1) * NW:(2 * KT + 2) * NW]
        mx = sb("mx", [P, NB, NCH])
        nmax = sb("nmax", [P, NB])
        m2 = sb("m2", [P, NB, 2], F16)
        rden = sb("rden", [P, NB])
        obuf = sb("obuf", [P, NB * C + CT * CHUNK])
        onorm = obuf[:, 0:NB * C].rearrange("p (a b) -> p a b", b=C)
        x1c = obuf[:, NB * C:].rearrange("p (t n) -> p t n", n=CHUNK)
        halo = CT * (ROWS + 2) * W
        zeros = obuf[:, 0:NB * C + CT * CHUNK - halo]
        hxs = [hx, obuf[:, NB * C + CT * CHUNK - halo:].rearrange("p (t r w) -> p t r w", t=CT, w=W)]
        xw = xin[:, 0].rearrange("p t n -> p (t n)")[:, 0:2 * NT * W].rearrange("p (u t w) -> p u t w", u=2, w=W)
        xgh, xgl = (onorm.rearrange("p a b -> p (a b)")[:, i * NT * W:(i + 1) * NT * W].bitcast(F16)
                    .rearrange("p (u t w) -> p u t w", u=2, w=W) for i in range(2))
        xg = x1c[:, 0, 0:NT * W].rearrange("p (t w) -> p t w", w=W)
        yo = xin[0:MO, 1].rearrange("p t n -> p (t n)")[:, 0:2 * NT * W].rearrange("p (u t w) -> p u t w", u=2, w=W)

        st1 = sb("st1", [P, CT, NCH, 6])
        rsum = sb("rsum", [P, CT, H])
        edge = sb("edge", [P, CT, H, 6])
        acol = onorm.rearrange("p a b -> p (a b)")[:, 0:CT * 7 * H].rearrange("p (t d h) -> p t d h", t=CT, d=7)
        wsum = sb("wsum", [P, CT, 7, 7])
        l1 = sb("l1", [P, 64])
        wk = sb("wk", [P, CT, 49])
        tmpw = sb("tmpw", [P, CT, 3, 49])
        uker = sb("uker", [P, CT, ULEN], F16)
        svec = sb("svec", [P, CT, 4])
        hbc = sb("hbc", [64, P])

        vker = flatp[:, 0:NG * SEG * 16 // 2].bitcast(F16)\
            .rearrange("p (g q j) -> p g q j", g=NG, q=SEG)
        sin = sb("sin", [P, NG, 2])
        sout = sb("sout", [MO, NG, 2])
        mrow = sb("mrow", [P, NG, NT])
        tmat = sb("tmat", [P, 2, SEG, TO, GC], F16)

        bank = [ctx.enter_context(nc.psum_tensor(f"bank{i}", [P, CHUNK], F32)) for i in range(8)]
        acc, sT, aux, tiny = bank[0:4], bank[4:6], bank[6:8], bank[5]

        s_load = sem("constants_loaded")
        s_wload = sem("projection_weights_loaded")
        s_lload = sem("layer1_weights_loaded")
        s_part = sem("waits_parted")
        s_zero = sem("scratch_pads_zeroed")
        s_set = sem("setup_chain")
        s_setp = sem("setup_product_ready")
        s_seta = sem("setup_activation_ready")
        s_xin = [sem("stat_chunk_loaded_even"), sem("stat_chunk_loaded_odd")]
        s_x0 = [sem(f"first_image_part_{h}_loaded") for h in range(NCH // 2)]
        s_xfree = sem("stat_chunk_free")
        s_poolset = sem("pool_setup")
        s_hx = [sem("halo_rows_loaded"), sem("halo_rows_loaded_odd")]
        s_high = sem("first_pools_high_ready")
        s_maxlow = sem("first_pools_max_low_ready")
        s_norm = sem("halo_rows_normalised")
        s_maxp = sem("pooled_maxima_ready")
        s_maxc = sem("pooled_maxima_chain")
        s_gcur = sem("pool_scalars_copied")
        s_pool = sem("pool_chain")
        s_cat = sem("pooled_rows_ready")
        s_qkps = sem("query_key_product_ready")
        s_qk32 = sem("query_key_scaled")
        s_qkadd = sem("query_key_complete")
        s_qkh = sem("query_key_high_ready")
        s_qk = sem("query_key_low_ready")
        s_vps = sem("value_product_ready")
        s_vhi = sem("value_high_ready")
        s_vlo = sem("value_low_ready")
        s_mps = sem("max_scores_ready")
        s_mfree = sem("max_scores_reduced")
        s_mchain = sem("row_maxima_chain")
        s_m2 = sem("row_maxima_ready")
        s_mrow = sem("row_maxima_turned")
        s_rows = sem("maxima_rows_stored")
        s_st = sem("scores_ready")
        s_exp = sem("exp_ready")
        s_lo = sem("exp_low_ready")
        s_pv = sem("value_step_done")
        s_acc = sem("sum_block_done")
        s_rden = sem("reciprocal_ready")
        s_on = sem("sum_block_normalised")
        s_turn = sem("outputs_turned")
        s_xr = sem("residual_loaded")
        s_xk = sem("residual_scaled")
        s_x1 = sem("x1_chunk_ready")
        s_x1o = sem("x1_chunk_stored")
        s_x1st = sem("x1_statistics_done")
        s_l1 = sem("layer1_chain")
        s_l1p = sem("layer1_product_ready")
        s_l1a = sem("layer1_activation_ready")
        s_usto = sem("kernels_stored")
        s_uld = sem("kernels_loaded")
        s_uldp = sem("kernels_loaded_by_pool")
        s_mr = sem("window_scales_ready")
        s_xw = [sem("window_rows_loaded_even"), sem("window_rows_loaded_odd")]
        s_xg = sem("window_normalised")
        s_xgh = sem("window_high_ready")
        s_xgl = sem("window_low_ready")
        s_tm = sem("band_matrices_ready")
        s_cv = sem("convolution_ready")
        s_y = sem("output_tile_ready")
        s_out = [sem("outputs_stored_even"), sem("outputs_stored_odd")]
        s_outp = [sem("outputs_stored_by_pool_even"), sem("outputs_stored_by_pool_odd")]

        block = ctx.enter_context(nc.Block())
        ts, ds = bass.ts, bass.ds

        def part(eng):
            eng.sem_inc(s_part, 1)

        def chain(eng, s, start, parted=False):
            def link(ins):
                link.count += 1
                ins.then_inc(s, 1)
                eng.wait_ge(s, start + link.count)
                if parted:
                    part(eng)
            link.count = 0
            return link

        N_SUM, N_MAX = 7, 3
        N_SUM0 = 4
        N_L1 = 60
        hops = {}
        pieces = [[(t, max(ROWS * g, TO * t - 3), min(ROWS * g + ROWS, TO * t - 3 + WIN)) for t in range(NT)
                   if max(ROWS * g, TO * t - 3) < min(ROWS * g + ROWS, TO * t - 3 + WIN)] for g in range(NCH)]
        stores = [CT * sum(len(p) for p in pieces[:g]) for g in range(NCH + 1)]
        U_LOADS_POOL = 7
        U_LOADS = WIN + 2 - U_LOADS_POOL
        Y_STORES = NT
        SP_STORES = 4
        POOL_STORES = Y_STORES - SP_STORES
        MAXSTEPS = NB * NCH

        xv = x.rearrange("b (t p) n -> b p t n", p=P)

        def first_image(eng, body):
            body(0, 0, 1, 0)
            with eng.Fori(0, NCH // 2 - 1) as h:
                body(h, 1, 0, 0)
                body(h + 1, 0, 0, 0)
            body(NCH // 2 - 1, 1, 0, 1)

        def stat_chunk(pair, odd, image):
            k = (B - 1) * odd + image - 1
            return k % 2, (B - 1) * pair + k // 2 + 1, 2 * (B - 1) * pair + k + 1

        def beside(layer1, b, feature_chunk):
            chunks = iter(range(NCH))
            layer1(b, lambda: feature_chunk(b + 1, next(chunks)))
            for j in chunks:
                feature_chunk(b + 1, j)

        def nothing():
            pass

        def windows(link, eng, op, kind, first, last, hx=hx, between=nothing):
            n = ROWS + 2 - first - last
            two = pairs[kind][:, :, 0:(n - 1) * W].rearrange("p t (r w) -> p t r w", w=W)
            cols2 = pairs[kind][:, :, 0:ROWS * (W + 1)].rearrange("p t (r w) -> p t r w", w=W + 1)
            three = threes[kind]
            inner = three[:, :, :, 1:W + 1]
            link(eng.tensor_tensor(two, hx[:, :, 0:n - 1, :], hx[:, :, 1:n, :], op))
            between()
            if first:
                link(eng.tensor_copy(inner[:, :, 0, :], two[:, :, 0, :]))
            if last:
                link(eng.tensor_copy(inner[:, :, ROWS - 1, :], two[:, :, n - 2, :]))
            link(eng.tensor_tensor(inner[:, :, first:first + n - 2, :], two[:, :, 0:n - 2, :], hx[:, :, 2:n, :], op))
            between()
            link(eng.tensor_tensor(cols2, three[:, :, :, 0:W + 1], three[:, :, :, 1:W + 2], op))
            between()
            ins = eng.tensor_tensor(pooled[kind][:].rearrange("p t (r w) -> p t r w", w=W),
                                    cols2[:, :, :, 0:W], three[:, :, :, 2:W + 2], op)
            if kind == 0:
                link(ins)
            return ins

        def load_kernels(eng, some, s_loaded):
            for k in some:
                eng.dma_start(vker[k::WIN].rearrange("c g q j -> c g (q j)"),
                              bass.AP(kern, WIN - 1 - k, [[ULEN, GC], [GC * ULEN, NG], [1, SEG * 16]]))\
                    .then_inc(s_loaded, 16)

        def store_y(eng, b, gi, u, some, s_stored):
            eng.wait_ge(s_y, 2 + b * NG + gi + 1)
            for t in some:
                m = min(TO, H - TO * t)
                eng.dma_start(bass.AP(out.tensor, b * (C * N) + gi * (GC * N) + t * TO * W,
                                      [[W, m], [N, GC], [1, W]]),
                              yo[0:m * GC, u, t, :]).then_inc(s_stored[u], 16)

        @block.vector
        def _(dve):
            V = nc.vector
            link = chain(dve, s_set, 0)
            V.memset(lnp[:], float(np.log(P_TOP))).then_inc(s_pv, 4)
            V.memset(epst[:], EPS).then_inc(s_xfree, 2)
            V.memset(m2[:], 0.0).then_inc(s_vlo, 4)
            V.memset(mx[:], 0.0).then_inc(s_mfree, 2)
            V.memset(uker[:], 0.0).then_inc(s_cv, 2)
            V.memset(nmax[:], 0.0).then_inc(s_y, 2)
            for s in (s_mrow, s_on, s_turn, s_qkadd, s_qk, s_xgh, s_xgl):
                dve.sem_inc(s, 1)
            link(V.memset(zeros, 0.0))
            hops["zeros"] = link.count
            link(V.memset(ones[:], 1.0))
            def image_statistics(b0, b1):
                for b in range(b0, b1):
                    for t in range(CT):
                        link(V.bn_aggr(me0[:, b * CT + t, :], st0[:, b, :, t, :]))
                some = slice(b0 * CT, b1 * CT)
                link(V.tensor_tensor(gn0[:, 0, some], me0[:, some, 0], me0[:, some, 0], ALU.mult))
                link(V.tensor_tensor(me0[:, some, 1], me0[:, some, 1], gn0[:, 0, some], ALU.add))
                hops["me0", b0] = link.count

            def image_scalars(b0, b1, turn):
                some = slice(b0 * CT, b1 * CT)
                gsum = tiny[:, 0:2 * B * CT].rearrange("p (i v) -> p i v", v=2)
                link(V.tensor_copy(gn0[:, 1, some], gsum[:, some, 0]))
                link(V.tensor_tensor(gn0[:, 2, some], gn0[:, 1, some], gn0[:, 1, some], ALU.mult))
                link(V.tensor_tensor(gn0[:, 3, some], gsum[:, some, 1], gn0[:, 2, some], ALU.subtract))
                hops["var0", b0] = link.count
                dve.wait_ge(s_seta, turn)
                link(V.reciprocal(gn0[:, 5, some], gn0[:, 4, some]))
                r0, mean0 = gn0[:, 5, some], gn0[:, 1, some]
                flat = gnp[:].rearrange("p b t v -> p (b t) v")[:, some]
                link(V.tensor_scalar(flat[:, :, 0], r0, XS, None, ALU.mult))
                link(V.scalar_tensor_tensor(flat[:, :, 1], mean0, -XS, r0, ALU.mult, ALU.mult))
                hops["gnp", b0] = link.count
                link(V.tensor_scalar(flat[:, :, 2], r0, small[:, 8:9], 1.0, ALU.mult, ALU.add))
                link(V.scalar_tensor_tensor(gn0[:, 6, some], mean0, small[:, 8:9], r0, ALU.mult, ALU.mult))
                for t in range(CT):
                    link(V.tensor_scalar(gnp[:, b0:b1, t, 3],
                                         gn0[:, 6, some].rearrange("p (b t) -> p t b", t=CT)[:, t, :],
                                         -1.0, small[:, 9 + t:10 + t], ALU.mult, ALU.add))

            dve.wait_ge(s_load, 16 * 3)
            link(V.tensor_copy(identh[:], ident))
            link(V.tensor_copy(maskc[:], cst[:, NT:NT + GC]))
            link(V.tensor_scalar(small[:, 8:9], alpha, -1.0, 1.0, ALU.mult, ALU.add))
            link(V.tensor_scalar(small[:, 9:11], col[:, BD:BD + CT], alpha, None, ALU.mult))
            dve.wait_ge(s_wload, 16)
            link(V.scalar_tensor_tensor(wabs, wraw, -1.0, wraw, ALU.mult, ALU.max))
            hops["wabs"] = link.count

            for h in range(NCH // 2):
                dve.wait_ge(s_x0[h], 16)
                for u in range(2):
                    for t in range(CT):
                        ins = V.bn_stats(st0[:, 0, h * 2 + u, t, :], x0[:, h, t, u * CHUNK:(u + 1) * CHUNK])
                link(ins)
            image_statistics(0, 1)
            dve.wait_ge(s_setp, 2)
            image_scalars(0, 1, 1)

            def set_up_weights():
                dve.wait_ge(s_setp, 1)
                link(V.tensor_scalar(wtot, bank[0][:, 0:C + 2 * C8], 1e-30, None, ALU.max))
                hops["wtot"] = link.count
                for i in range(2):
                    span = wtot[:, C + i * C8:C + (i + 1) * C8]
                    link(V.tensor_reduce(small[:, i:i + 1], span, X, ALU.max))
                    link(V.tensor_scalar(span, span, 0.0, small[:, i:i + 1], ALU.mult, ALU.add))
                    link(V.tensor_reduce(small[:, 2 + i:3 + i], bbrow[:, i * C8:(i + 1) * C8], X, ALU.max,
                                         apply_absolute_value=True))
                    link(V.scalar_tensor_tensor(small[:, 4 + i:5 + i], small[:, i:i + 1], GN_MAX,
                                                small[:, 2 + i:3 + i], ALU.mult, ALU.add))
                    link(V.reciprocal(small[:, 6 + i:7 + i], small[:, 4 + i:5 + i]))
                    q = slice(i * C8, (i + 1) * C8)
                    for half in (q, slice(2 * C8 + i * C8, 2 * C8 + (i + 1) * C8)):
                        link(V.scalar_tensor_tensor(qk_scale[half], small[half, i:i + 1], QK_TOP / (XS * WS),
                                                    small[half, 6 + i:7 + i], ALU.mult, ALU.mult))
                    link(V.scalar_tensor_tensor(qk_bias[q], col[q, BBC:BBC + 1], QK_TOP,
                                                small[q, 6 + i:7 + i], ALU.mult, ALU.mult))
                link(V.scalar_tensor_tensor(escale[:], small[:, 4:5], QK_TOP ** -2, small[:, 5:6],
                                            ALU.mult, ALU.mult))
                link(V.reciprocal(wscale, wtot))
                for k in range(KT):
                    link(V.scalar_tensor_tensor(wabs[:, k, :], wraw[:, k, :], WS / 9.0 if k < CT else WS,
                                                wscale, ALU.mult, ALU.mult))
                for high, low, span in ((wh[:], wl[:], wabs[:, :, 0:C]),
                                        (wqk[:, :, 0:2 * C8], wqk[:, :, 2 * C8:], wabs[:, :, C:])):
                    link(V.tensor_copy(high, span))
                    link(V.tensor_tensor(low, span, high, ALU.subtract))
                hops["weights"] = link.count
                dve.wait_ge(s_setp, 3)
                link(V.tensor_scalar(vdesc[:], bank[1][:, 0:CT], alpha, 1.0 / DV_SCALE, ALU.mult, ALU.mult))
                hops["vdesc"] = link.count

            def pool_maxima(b, q, first, last, between):
                n = b * NCH + q
                dve.wait_ge(s_norm, CT * (n + 1))
                dve.wait_ge(s_cat, n)
                link = chain(dve, s_maxc, n * N_MAX + 2 * b + (0 if first else 1))
                windows(link, V, ALU.max, 1, first, last, between=between).then_inc(s_maxp, 1)
                assert link.count == N_MAX + first + last, link.count

            def feature_chunk(b, j, between=nothing):
                dve.wait_ge(s_qk32, b * NCH + j + 1)
                V.scalar_tensor_tensor(qk32[:], bank[0][64:128, :], qk_scale[64:128, :], qk32[:],
                                       ALU.mult, ALU.add).then_inc(s_qkadd, 1)
                between()

                def value_low(u):
                    dve.wait_ge(s_vhi, b * KEYT + j * 4 + u + 1)
                    V.scalar_tensor_tensor(vl[:, j * 4 + u, :], bank[1 + u][:, 0:C], DV_SHIFT,
                                           vh[:, j * 4 + u, 0:C], ALU.mult, ALU.subtract)\
                        .then_inc(s_vlo, 1)

                value_low(0)
                dve.wait_ge(s_qkh, b * NCH + j + 1)
                cs = ts(j, CHUNK)
                V.tensor_tensor(bq[32:64, cs], qk32[0:32], bq[0:32, cs], ALU.subtract)
                V.tensor_copy(bq[64:96, cs], bq[0:32, cs])
                V.tensor_copy(ck[32:64, cs], ck[0:32, cs])
                V.tensor_tensor(ck[64:96, cs], qk32[32:64], ck[0:32, cs], ALU.subtract).then_inc(s_qk, 1)
                for u in range(1, 4):
                    value_low(u)

            def first_chunk(pair, odd, first, last):
                q = pair * 2 + odd
                dve.wait_ge(s_norm, CT * (q + 1))
                if not first:
                    dve.wait_ge(s_high, 2 * q)
                    dve.wait_ge(s_maxlow, q)
                windows(chain(dve, s_maxc, q * N_MAX + 1 - first), V, ALU.max, 1, first, last, hxs[odd])\
                    .then_inc(s_maxp, 1)

                def statistics(image):
                    u, loads, _ = stat_chunk(pair, odd, image)
                    dve.wait_ge(s_xin[u], 16 * loads)
                    for t in range(CT):
                        ins = V.bn_stats(st0[:, image, q, t, :], xin[:, u, t, :])
                    ins.then_inc(s_xfree, 1)

                statistics(1)
                dve.wait_ge(s_maxp, q + 1)
                dve.wait_ge(s_high, 2 * q + 1)
                V.tensor_tensor(catl[:, CT:KT, ts(q, CHUNK)], pooled[1][:], cath[:, CT:KT, ts(q, CHUNK)],
                                ALU.subtract).then_inc(s_maxlow, 1)
                if first:
                    set_up_weights()
                statistics(2)
                if first:
                    statistics(3)
                else:
                    feature_chunk(0, q - 1, lambda: statistics(3))

            def max_step(n, dst, e):
                dve.wait_ge(s_mps, n + 1)
                V.tensor_reduce(dst, aux[e][:], X, ALU.max).then_inc(s_mfree, 1)

            def max_pass(b):
                with dve.Fori(0, NB) as nb:
                    for c in range(NCH):
                        max_step(b * N // 16 + nb * NCH + c, mx[:, nb, c:c + 1], c % 2)

            def max_finish(r):
                dve.wait_ge(s_mfree, 2 + MAXSTEPS * (r + 1))
                dve.wait_ge(s_mrow, 1 + r)
                V.tensor_reduce(nmax[:], mx[:], X, ALU.max, negate=True).then_inc(s_mchain, 1)
                dve.wait_ge(s_mchain, 2 * r + 1)
                V.tensor_scalar(m2[:, :, 0], nmax[:], 1.0 / MAXROW, None, ALU.mult).then_inc(s_mchain, 1)
                dve.wait_ge(s_mchain, 2 * r + 2)
                V.scalar_tensor_tensor(m2[:, :, 1], nmax[:], 1.0 / MAXROW, m2[:, :, 0], ALU.mult, ALU.subtract)\
                    .then_inc(s_m2, 1)

            def low_part(s, i):
                dve.wait_ge(s_exp, s + 1)
                V.tensor_tensor(pl[i], p32[i], ph[i], ALU.subtract).then_inc(s_lo, 1)

            def finish(b, g, r, between=nothing):
                dve.wait_ge(s_xr, 16 * (r + 1))
                for t in range(CT):
                    V.tensor_scalar(xin[:, 0, t, :], xin[:, 0, t, :], gnp[:, b, t, 2:3], gnp[:, b, t, 3:4],
                                    ALU.mult, ALU.add).then_inc(s_xk, 1)
                between()
                dve.wait_ge(s_xk, CT * (r + 1))
                for t in range(CT):
                    dve.wait_ge(s_turn, CT * r + t + 2)
                    V.scalar_tensor_tensor(x1c[:, t, :], aux[t][:], vdesc[:, t:t + 1], xin[:, 0, t, :],
                                           ALU.mult, ALU.add).then_inc(s_x1, 1)
                    between()
                dve.wait_ge(s_x1, CT * (r + 1))
                for t in range(CT):
                    V.bn_stats(st1[:, t, g, :], x1c[:, t, :])
                between()
                rows4 = x1c.rearrange("p t (r w) -> p t r w", w=W)
                V.tensor_reduce(rsum[:, :, ds(g * ROWS, ROWS)], rows4, X, ALU.add)
                between()
                V.tensor_copy(edge[:, :, ds(g * ROWS, ROWS), 0:3], rows4[:, :, :, 0:3])
                V.tensor_copy(edge[:, :, ds(g * ROWS, ROWS), 3:6], rows4[:, :, :, W - 3:W]).then_inc(s_x1st, 1)

            def group(b, g, with_finish, with_next, pool_next):
                r = b * NCH + g
                s0 = r * KEYT

                with dve.Fori(0, 4) as i:
                    for u in range(4):
                        if with_next:
                            for e in range(2):
                                max_step((r + 1) * MAXSTEPS + i * 8 + 2 * u + e, mx[:, i, 2 * u + e:2 * u + e + 1], e)
                        low_part(s0 + i * 4 + u + 2, (u + 2) % 4)

                step = iter(range(KEYT // 2 + 2, KEYT + 2 if with_next else KEYT))

                def next_low():
                    s = next(step)
                    low_part(s0 + s, s % 4)
                if with_next:
                    max_finish(r + 1)
                next_low()
                if with_finish:
                    finish(b, g - 1, r - 1, next_low)
                next_low()
                if pool_next:
                    pool_maxima(b + 1, g, int(not with_finish), int(not with_next), next_low)
                for s in step:
                    if s < KEYT + 1:
                        low_part(s0 + s, s % 4)
                dve.wait_ge(s_on, 1 + NB * r)
                for nb in range(NB):
                    if nb < NB - 1:
                        dve.wait_ge(s_acc, (NB - 1) * r + nb + 1)
                    else:
                        dve.wait_ge(s_pv, 4 + s0 + KEYT)
                    V.reciprocal(rden[:, nb:nb + 1], acc[nb][:, C:C + 1]).then_inc(s_rden, 1)
                if with_next:
                    low_part(s0 + KEYT + 1, 1)

            def attention(b, pool_next):
                max_finish(b * NCH)
                for u in range(2):
                    low_part(b * NCH * KEYT + u, u)
                group(b, 0, False, True, pool_next)
                with dve.Fori(1, NCH - 1) as g:
                    group(b, g, True, True, pool_next)
                group(b, NCH - 1, True, False, pool_next)
                finish(b, NCH - 1, b * NCH + NCH - 1)

            def layer1(b, between):
                link = chain(dve, s_l1, b * N_L1)
                T, S, M, A, SUB = V.tensor_tensor, V.scalar_tensor_tensor, ALU.mult, ALU.add, ALU.subtract

                def cols(a, n=1):
                    return l1[:, a:a + n]
                dve.wait_ge(s_x1st, NCH * (b + 1))
                part(dve)
                me = cols(0, 4).rearrange("p (t v) -> p t v", v=2)
                for t in range(CT):
                    link(V.bn_aggr(me[:, t, :], st1[:, t, :, :]))
                    part(dve)
                link(T(cols(4, 2), me[:, :, 0], me[:, :, 0], M))
                link(T(me[:, :, 1], me[:, :, 1], cols(4, 2), A))
                hops["me"] = link.count
                between()
                link(V.tensor_copy(acol[:, :, 3, :], rsum[:]))
                for d, e in ((4, 0), (5, 1), (6, 2), (2, 5), (1, 4), (0, 3)):
                    near = d - 1 if d > 3 else d + 1
                    link(T(acol[:, :, d, :], acol[:, :, near, :], edge[:, :, :, e], SUB))
                link(V.tensor_reduce(wsum[:, :, :, 3], acol[:], X, A))
                for e, row_out in ((2, 0), (1, 1), (0, 2), (4, H - 1), (5, H - 2), (6, H - 3)):
                    near = e + 1 if e < 3 else e - 1
                    link(T(wsum[:, :, :, e], wsum[:, :, :, near], acol[:, :, :, row_out], SUB))
                between()
                dve.wait_ge(s_l1p, 4 * b + 1)
                link(V.tensor_copy(cols(6, 2), tiny[:, 0:4].rearrange("p (t v) -> p t v", v=2)[:, :, 0]))
                link(T(cols(8, 2), cols(6, 2), cols(6, 2), M))
                link(T(cols(10, 2), tiny[:, 0:4].rearrange("p (t v) -> p t v", v=2)[:, :, 1], cols(8, 2), SUB))
                hops["var"] = link.count
                mean, std, r, nr = cols(6, 2), cols(12, 2), cols(14, 2), cols(22, 2)
                dve.wait_ge(s_l1a, 4 * b + 1)
                link(V.reciprocal(r, std))
                link(V.tensor_scalar(nr, r, -1.0 / N, None, M))
                flat = wsum[:].rearrange("p t d e -> p t (d e)")
                for t in range(CT):
                    link(S(flat[:, t, :], cnt, mean[:, t:t + 1], flat[:, t, :], M, SUB))
                    link(T(tmpw[:, t], w7s[:, t], flat[:, t:t + 1, :].broadcast_to([P, 3, 49]), M))
                mk = cols(16, 6).rearrange("p (t k) -> p t k", k=3)
                link(V.tensor_reduce(mk, tmpw[:], X, A))
                mean_k = cols(24, 6).rearrange("p (t k) -> p t k", k=3)
                bias_k = col[:, DWB:DWB + 6].rearrange("p (t k) -> p t k", k=3)
                for t in range(CT):
                    link(S(mean_k[:, t, :], mk[:, t, :], nr[:, t:t + 1], bias_k[:, t, :], M, A))
                hops["mean_k"] = link.count
                between()
                dve.wait_ge(s_l1p, 4 * b + 2)
                link(T(cols(30, 2), tiny[:, 8:10], col[:, BPW:BPW + 2], A))
                hops["g"] = link.count
                between()
                dve.wait_ge(s_l1p, 4 * b + 3)

                def hid(a):
                    return l1[0:64, a:a + 1]
                link(T(hid(32), tiny[0:64, 16:17], col[0:64, BA1:BA1 + 1], A))
                link(V.tensor_scalar(hid(33), hid(32), 20.0, None, ALU.min))
                hops["hid"] = link.count
                dve.wait_ge(s_l1a, 4 * b + 2)
                link(S(hid(35), hid(34), 2.0, hid(34), A, M))
                link(V.tensor_scalar(hid(36), hid(35), 2.0, None, A))
                link(V.reciprocal(hid(37), hid(36)))
                link(T(hid(38), hid(35), hid(37), M))
                link(T(hid(39), hid(38), hid(32), M))
                link(V.tensor_scalar(hbc[:], ones[0:64, :], hid(39), None, M))
                hops["hbc"] = link.count
                between()
                dve.wait_ge(s_l1p, 4 * b + 4)
                link(T(cols(40, 3), tiny[:, 24:27], ba2r, A))
                link(V.tensor_reduce(cols(43), cols(40, 3), X, ALU.max, negate=True))
                hops["logits"] = link.count
                dve.wait_ge(s_l1a, 4 * b + 3)
                link(V.tensor_reduce(cols(47), cols(44, 3), X, A))
                link(V.reciprocal(cols(48), cols(47)))
                link(V.tensor_scalar(cols(49, 3), cols(44, 3), cols(48), None, M))
                link(V.tensor_scalar(wk[:], w7s[:, :, 0, :], cols(49), None, M))
                for k in (1, 2):
                    link(S(wk[:], w7s[:, :, k, :], cols(49 + k), wk[:], M, A))
                link(T(wk[:, :, 24], wk[:, :, 24], std, A))
                weighted = cols(56, 6).rearrange("p (t k) -> p t k", k=3)
                link(T(weighted, bias_k, cols(49, 3).unsqueeze(1).broadcast_to([P, CT, 3]), M))
                link(V.tensor_reduce(cols(62, 2), weighted, X, A))
                link(T(svec[:, :, 3], cols(62, 2), mean, A))
                link(V.tensor_copy(svec[:, :, 0], mean))
                link(V.tensor_scalar(svec[:, :, 1], r, XS, None, M))
                link(V.tensor_reduce(cols(52, 2), wk[:], X, ALU.max, apply_absolute_value=True))
                link(V.reciprocal(cols(54, 2), cols(52, 2)))
                link(V.tensor_scalar(svec[:, :, 2], cols(52, 2), 1.0 / (KW * XS), None, M))
                hops["svec"] = link.count
                for t in range(CT):
                    link(V.tensor_scalar(wk[:, t, :], wk[:, t, :], cols(54 + t), KW, M, M))
                hops["wk"] = link.count
                dve.wait_ge(s_l1a, 4 * b + 4)
                uk = uker[:, :, 0:SEG * 16].rearrange("p t (q j) -> p t q j", j=16)[:, :, :, 9:16]
                for t in range(CT):
                    link(T(uk[:, t, TAPS:SEG], wk[:, t, :].rearrange("p (d e) -> p d e", e=7),
                           uk[:, t, 0:TAPS], SUB))
                part(dve)
                assert link.count == N_L1, link.count

            def convolution(b, with_max):
                dve.wait_ge(s_uld, 16 * U_LOADS * (b + 1))
                dve.wait_ge(s_uldp, 16 * U_LOADS_POOL * (b + 1))
                V.tensor_tensor(mrow[:], sin[:, :, 1:2].broadcast_to([P, NG, NT]),
                                cst[:, 0:NT].unsqueeze(1).broadcast_to([P, NG, NT]), ALU.mult).then_inc(s_mr, 1)
                dve.wait_ge(s_mr, b + 1)
                part(dve)

                def prepare(gi, u, loads):
                    n = b * NG + gi
                    dve.wait_ge(s_xw[u], 16 * (b * (NG // 2) + loads))
                    dve.wait_ge(s_xgh, 1 + n)
                    dve.wait_ge(s_xgl, 1 + n)
                    V.scalar_tensor_tensor(xg[:], xw[:, u], sin[:, gi, 0:1],
                                           mrow[:, gi, :].unsqueeze(2).broadcast_to([P, NT, W]),
                                           ALU.subtract, ALU.mult).then_inc(s_xg, 1)
                    dve.wait_ge(s_cv, n + 1)
                    V.tensor_tensor(tmat[:, u], vker[:, gi, :, 0:TO].unsqueeze(3).broadcast_to([P, SEG, TO, GC]),
                                    maskc[:].unsqueeze(1).unsqueeze(1).broadcast_to([P, SEG, TO, GC]),
                                    ALU.mult).then_inc(s_tm, 1)
                    dve.wait_ge(s_xgh, n + 2)
                    V.tensor_tensor(xgl[:, u], xg[:], xgh[:, u], ALU.subtract).then_inc(s_xgl, 1)

                mxs = mx[:].rearrange("p n c -> p (n c)")

                def maxima(gi, u):
                    if with_max:
                        max_step((b + 1) * NCH * MAXSTEPS + gi, mxs[:, ds(gi, 1)], u)

                prepare(0, 0, 1)
                with dve.Fori(0, NG // 2 - 1) as h:
                    prepare(h * 2 + 1, 1, h + 1)
                    maxima(h * 2, 0)
                    prepare(h * 2 + 2, 0, h + 2)
                    maxima(h * 2 + 1, 1)
                prepare(NG - 1, 1, NG // 2)
                maxima(NG - 2, 0)
                maxima(NG - 1, 1)

            dve.wait_ge(s_poolset, 4)
            first_image(dve, first_chunk)
            dve.wait_ge(s_xfree, 2 + (B - 1) * NCH)
            image_statistics(1, B)
            feature_chunk(0, NCH - 1)
            dve.wait_ge(s_setp, 4)
            image_scalars(1, B, 2)
            max_pass(0)
            dve.wait_ge(s_lload, 16 * 4)
            with dve.Fori(0, B - 1) as b:
                attention(b, True)
                beside(layer1, b, feature_chunk)
                convolution(b, True)
            attention(B - 1, False)
            layer1(B - 1, nothing)
            convolution(B - 1, False)

        @block.scalar
        def _(act):
            A = nc.scalar.activation

            def feature_chunk(b, j):
                cs = ts(j, CHUNK)
                act.wait_ge(s_qkps, b * NCH + j + 1)
                act.wait_ge(s_qk, 1 + b * NCH + j)
                A(qk32[:], bank[0][0:64, :], ACT.Identity, bias=qk_bias[:], scale=qk_scale[0:64, :]).then_inc(s_qk32, 1)

                def value_high(u):
                    act.wait_ge(s_vps, b * KEYT + j * 4 + u + 1)
                    A(vh[:, j * 4 + u, 0:C], bank[1 + u][:, 0:C], ACT.Copy, scale=DV_SHIFT).then_inc(s_vhi, 1)

                value_high(0)
                act.wait_ge(s_qkadd, b * NCH + j + 2)
                A(bq[0:32, cs], qk32[0:32], ACT.Copy)
                A(ck[0:32, cs], qk32[32:64], ACT.Copy).then_inc(s_qkh, 1)
                for u in range(1, 4):
                    value_high(u)

            def normalise(pair, odd, first, last):
                act.wait_ge(s_hx[odd], 16 * CT * (pair + 1))
                for t in range(CT):
                    rowsx = hxs[odd][:, t, 0:ROWS + 2 - first - last, :]
                    A(rowsx, rowsx, ACT.Identity, bias=gnp[:, 0, t, 1:2], scale=gnp[:, 0, t, 0:1]).then_inc(s_norm, 1)

            def first_chunk(pair, odd, first, last):
                q = pair * 2 + odd
                if first:
                    normalise(0, 0, 1, 0)
                if not last:
                    normalise(pair + odd, 1 - odd, 0, 0)
                act.wait_ge(s_maxp, q + 1)
                A(cath[:, CT:KT, ts(q, CHUNK)], pooled[1][:], ACT.Copy).then_inc(s_high, 1)
                act.wait_ge(s_pool, N_SUM0 * (q + 1) + 1 + last)
                A(cath[:, 0:CT, ts(q, CHUNK)], pooled[0][:], ACT.Copy).then_inc(s_high, 1)
                if not first:
                    feature_chunk(0, q - 1)

            def exp_step(s, i):
                act.wait_ge(s_st, s + 1)
                act.wait_ge(s_pv, s + 1)
                A(ph[i], sT[i % 2][:], ACT.Exp, bias=lnp[:], scale=escale[:])
                A(p32[i], sT[i % 2][:], ACT.Exp, bias=lnp[:], scale=escale[:]).then_inc(s_exp, 1)

            def store_rows(r, g):
                act.wait_ge(s_mrow, r + 2)
                A(bq[96:98, ts(g, CHUNK)], aux[0][96:98, :], ACT.Copy).then_inc(s_rows, 1)

            def group(b, g, with_next):
                r = b * NCH + g
                s0 = r * KEYT
                with act.Fori(0, 7) as i:
                    for u in range(4):
                        exp_step(s0 + i * 4 + u + 2, (u + 2) % 4)
                if with_next:
                    store_rows(r + 1, g + 1)
                for u in range(2):
                    exp_step(s0 + 28 + u + 2, (u + 2) % 4)
                if with_next:
                    for u in range(2):
                        exp_step(s0 + KEYT + u, u)
                act.wait_ge(s_turn, 1 + CT * r)
                for nb in range(NB):
                    act.wait_ge(s_rden, NB * r + nb + 1)
                    A(onorm[:, nb, :], acc[nb][:, 0:C], ACT.Copy, scale=rden[:, nb:nb + 1]).then_inc(s_on, 1)

            def attention(b):
                store_rows(b * NCH, 0)
                for u in range(2):
                    exp_step(b * NCH * KEYT + u, u)
                with act.Fori(0, NCH - 1) as g:
                    group(b, g, True)
                group(b, NCH - 1, False)

            def layer1(b, between):
                c0 = b * N_L1
                between()
                between()
                act.wait_ge(s_l1, c0 + hops["var"])
                A(l1[:, 12:14], l1[:, 10:12], ACT.Sqrt, bias=epst[:]).then_inc(s_l1a, 1)
                between()
                between()
                act.wait_ge(s_l1, c0 + hops["hid"])
                A(l1[0:64, 34:35], l1[0:64, 33:34], ACT.Exp).then_inc(s_l1a, 1)
                between()
                act.wait_ge(s_l1, c0 + hops["logits"])
                A(l1[:, 44:47], l1[:, 40:43], ACT.Exp, bias=l1[:, 43:44]).then_inc(s_l1a, 1)
                act.wait_ge(s_l1, c0 + hops["wk"])
                uk = uker[:, :, 0:SEG * 16].rearrange("p t (q j) -> p t q j", j=16)[:, :, :, 9:16]
                for t in range(CT):
                    ins = A(uk[:, t, 0:TAPS], wk[:, t, :].rearrange("p (d e) -> p d e", e=7), ACT.Copy)
                ins.then_inc(s_l1a, 1)

            def high_part(b, gi, u):
                n = b * NG + gi
                act.wait_ge(s_xg, n + 1)
                act.wait_ge(s_cv, n + 1)
                A(xgh[:, u], xg[:], ACT.Copy).then_inc(s_xgh, 1)

            def evacuate(b, gi, h, u, first=False):
                n = b * NG + gi
                act.wait_ge(s_cv, 2 + n + 1)
                if not first:
                    act.wait_ge(s_out[u], 16 * SP_STORES * (b * (NG // 2) + h))
                    act.wait_ge(s_outp[u], 16 * POOL_STORES * (b * (NG // 2) + h))
                A(yo[:, u], acc[u][0:MO, 0:NT * W].rearrange("p (t w) -> p t w", w=W), ACT.Identity,
                  bias=sout[:, gi, 1:2], scale=sout[:, gi, 0:1]).then_inc(s_y, 1)

            def convolution(b):
                act.wait_ge(s_uld, 16 * U_LOADS * (b + 1))
                for u in range(2):
                    high_part(b, u, u)
                for u in range(2):
                    evacuate(b, u, 0, u, True)
                    high_part(b, u + 2, u)
                with act.Fori(1, NG // 2 - 1) as h:
                    for u in range(2):
                        evacuate(b, h * 2 + u, h, u)
                        high_part(b, h * 2 + u + 2, u)
                for u in range(2):
                    evacuate(b, NG - 2 + u, NG // 2 - 1, u)

            def deviations(b0, b1):
                act.wait_ge(s_set, hops["var0", b0])
                some = slice(b0 * CT, b1 * CT)
                A(gn0[:, 4, some], gn0[:, 3, some], ACT.Sqrt, bias=epst[:]).then_inc(s_seta, 1)

            deviations(0, 1)
            act.wait_ge(s_set, hops["gnp", 0])
            first_image(act, first_chunk)
            feature_chunk(0, NCH - 1)
            deviations(1, B)
            act.wait_ge(s_zero, 16 * 4 * B)
            with act.Fori(0, B - 1) as b:
                attention(b)
                beside(layer1, b, feature_chunk)
                convolution(b)
            attention(B - 1)
            layer1(B - 1, nothing)
            convolution(B - 1)

        @block.tensor
        def _(pe):
            MM = nc.tensor.matmul
            NW = C + 2 * C8

            def product3(out_ap, stat, mov, start, stop):
                terms = [(s, m) for sh, sl, mh, ml in zip(*stat, *mov) for s, m in ((sh, mh), (sh, ml), (sl, mh))]
                for i, (s, m) in enumerate(terms):
                    ins = MM(out_ap, s, m, start=start and i == 0, stop=stop and i == len(terms) - 1)
                return ins

            def feature_chunk(b, j, first=False):
                after_attention = not first and j == 0
                if after_attention:
                    pe.wait_ge(s_on, 1 + NB * NCH * b)
                cs = ts(j, CHUNK)
                pe.wait_ge(s_cat, b * NCH + j + 1)
                if first:
                    pe.wait_ge(s_maxlow, j + 1)
                pe.wait_ge(s_qkadd, 1 + b * NCH + j)
                ks = range(KT)
                for k in ks:
                    if k < KT - 1:
                        MM(bank[0][:], wqk[:, k, :], cath[:, k, cs], start=(k == 0), stop=False)
                    MM(bank[0][0:64, :], wqk[:, k, 0:64], catl[:, k, cs], start=False, stop=False)
                MM(bank[0][:], wqk[:, KT - 1, :], cath[:, KT - 1, cs], start=False, stop=True).then_inc(s_qkps, 1)
                for u in range(4):
                    if after_attention and u == 3:
                        pe.wait_ge(s_exp, NCH * KEYT * b)
                    pe.wait_ge(s_vlo, b * KEYT + j * 4 + u + 1)
                    tc = ts(j * 4 + u, P)
                    product3(bank[1 + u][:, 0:C], ([cath[:, k, tc] for k in ks], [catl[:, k, tc] for k in ks]),
                             ([wh[:, k, 0:C] for k in ks], [wl[:, k, 0:C] for k in ks]), True, True)\
                        .then_inc(s_vps, 1)

            def max_block(n, q, k, e):
                pe.wait_ge(s_mfree, n + 1)
                MM(aux[e][:], bq[0:96, q], ck[0:96, k], start=True, stop=True).then_inc(s_mps, 1)

            def max_pass(b):
                with pe.Fori(0, NB) as nb:
                    for c in range(NCH):
                        max_block(b * NCH * MAXSTEPS + nb * NCH + c, ts(nb, P), ts(c, CHUNK), c % 2)

            def turn_maxima(r):
                pe.wait_ge(s_m2, r + 1)
                for nb in range(NB):
                    ins = MM(aux[0][96:98, nb * P:(nb + 1) * P], m2[:, nb, :], identh[:], start=True, stop=True)
                ins.then_inc(s_mrow, 1)

            def scores(g, t, i):
                MM(sT[i % 2][:], ck[0:98, ts(t, P)], bq[0:98, ts(g, CHUNK)], start=True, stop=True).then_inc(s_st, 1)

            def group(b, g, with_finish, with_next, first_group):
                r = b * NCH + g
                s0 = r * KEYT

                def step(i, u, first, last, maxima):
                    s = s0 + i * 4 + u
                    if not last or u < 2:
                        pe.wait_ge(s_exp, s + 1)
                        scores(g, i * 4 + u + 2, u)
                    elif with_next:
                        pe.wait_ge(s_exp, s + 1)
                        if u == 2:
                            pe.wait_ge(s_rows, r + 2)
                        scores(g + 1, u - 2, u)
                    pe.wait_ge(s_lo, s + 1)
                    start, stop = first and u == 0, last and u == 3
                    t = i * 4 + u
                    for nb in range(NB):
                        if maxima and nb % 2 == 0:
                            e = nb // 2
                            max_block((r + 1) * MAXSTEPS + i * 8 + 2 * u + e, ds((g + 1) * CHUNK + i * P, P),
                                      ts(2 * u + e, CHUNK), e)
                        if start and not first_group:
                            pe.wait_ge(s_on, NB * (r - 1) + nb + 2)
                        q = slice(nb * P, (nb + 1) * P)
                        MM(acc[nb][:, 0:C + 1], ph[u][:, q], vh[:, t, 0:C + 1], start=start, stop=False)
                        MM(acc[nb][:, 0:C], ph[u][:, q], vl[:, t, :], start=False, stop=False)
                        ins = MM(acc[nb][:, 0:C + 1], pl[u][:, q], vh[:, t, 0:C + 1], start=False, stop=stop)
                        if stop and nb < NB - 1:
                            ins.then_inc(s_acc, 1)
                    ins.then_inc(s_pv, 1)

                for u in range(4):
                    step(0, u, True, False, with_next)
                with pe.Fori(1, 4) as i:
                    for u in range(4):
                        step(i, u, False, False, with_next)
                if with_finish:
                    turn_sums(r - 1, (r + 2) if with_next else (r + 1))
                with pe.Fori(4, 7) as i:
                    for u in range(4):
                        step(i, u, False, False, False)
                if with_next:
                    if with_finish:
                        pe.wait_ge(s_x1, CT * r)
                    else:
                        pe.wait_ge(s_mfree, 2 + MAXSTEPS * (r + 2))
                    turn_maxima(r + 1)
                for u in range(4):
                    step(7, u, False, True, False)

            def turn_sums(r, groups):
                pe.wait_ge(s_on, 1 + NB * (r + 1))
                pe.wait_ge(s_mfree, 2 + MAXSTEPS * groups)
                for t in range(CT):
                    for nb in range(NB):
                        ins = nc.tensor.transpose(aux[t][:, nb * P:(nb + 1) * P], onorm[:, nb, t * P:(t + 1) * P],
                                                  ident)
                    ins.then_inc(s_turn, 1)

            def attention(b):
                pe.wait_ge(s_mfree, 2 + MAXSTEPS * (b * NCH + 1))
                turn_maxima(b * NCH)
                pe.wait_ge(s_vlo, 4 + KEYT * (b + 1))
                pe.wait_ge(s_y, 2 + NG * b)
                pe.wait_ge(s_rows, b * NCH + 1)
                for u in range(2):
                    scores(0, u, u)
                group(b, 0, False, True, True)
                with pe.Fori(1, NCH - 1) as g:
                    group(b, g, True, True, False)
                group(b, NCH - 1, True, False, False)
                turn_sums(b * NCH + NCH - 1, b * NCH + NCH)

            def layer1(b, between):
                c0 = b * N_L1
                between()
                between()
                pe.wait_ge(s_exp, NCH * KEYT * (b + 1))
                pe.wait_ge(s_l1, c0 + hops["me"])
                MM(tiny[:, 0:4], gmat, l1[:, 0:4], start=True, stop=True).then_inc(s_l1p, 1)
                between()
                pe.wait_ge(s_l1, c0 + hops["mean_k"])
                for o in range(CT):
                    for i in range(3 * CT):
                        k, t = i // CT, i % CT
                        ins = MM(tiny[:, 8 + o:9 + o], wpws[:, i, o * P:(o + 1) * P],
                                 l1[:, 24 + t * 3 + k:25 + t * 3 + k], start=(i == 0), stop=(i == 3 * CT - 1))
                ins.then_inc(s_l1p, 1)
                between()
                pe.wait_ge(s_l1, c0 + hops["g"])
                for o in range(CT):
                    ins = MM(tiny[0:64, 16:17], wa1s[:, o, :], l1[:, 30 + o:31 + o], start=(o == 0), stop=(o == CT - 1))
                ins.then_inc(s_l1p, 1)
                between()
                pe.wait_ge(s_l1, c0 + hops["hbc"])
                MM(tiny[:, 24:27], hbc[:], wa2s[:], start=True, stop=True).then_inc(s_l1p, 1)

            def convolve(b, gi, u):
                n = b * NG + gi
                pe.wait_ge(s_y, n + 1)
                pe.wait_ge(s_xgh, n + 2)
                pe.wait_ge(s_tm, n + 1)
                pe.wait_ge(s_xgl, n + 2)
                out3 = acc[u][0:MO, 0:NT * W].rearrange("p (t w) -> p t w", w=W)
                order = [3, 2, 4, 1, 5, 0, 6]
                for d in order:
                    lo, hi = max(0, 3 - d), W - max(0, d - 3)
                    for i, (q, xp) in enumerate(((d, xgh), (d, xgl), (TAPS + d, xgh))):
                        ins = MM(out3[:, :, lo:hi], tmat[:, u, q].rearrange("p m c -> p (m c)"),
                                 xp[:, u, :, lo + d - 3:hi + d - 3],
                                 start=(d == 3 and i == 0), stop=(d == 6 and i == 2))
                ins.then_inc(s_cv, 1)

            def convolution(b, with_max):
                if with_max:
                    pe.wait_ge(s_qk, 1 + NCH * (b + 2))
                    pe.wait_ge(s_x1, CT * NCH * (b + 1))
                pe.wait_ge(s_vlo, 4 + KEYT * (b + 1 + with_max))
                part(pe)
                with pe.Fori(0, NB) as nb, pe.Fori(0, NCH // 2) as h:
                    for u in range(2):
                        gi = nb * NCH + h * 2 + u
                        if with_max:
                            max_block((b + 1) * NCH * MAXSTEPS + gi, ts(nb, P), ts(h * 2 + u, CHUNK), u)
                        convolve(b, gi, u)

            def group_means(b0, b1):
                pe.wait_ge(s_set, hops["me0", b0])
                MM(tiny[:, 2 * b0 * CT:2 * b1 * CT], gmat, me0[:, b0 * CT:b1 * CT].rearrange("p i v -> p (i v)"),
                   start=True, stop=True).then_inc(s_setp, 1)

            pe.wait_ge(s_set, hops["wabs"])
            for k in range(KT):
                ins = MM(bank[0][:, 0:NW], ones[:], wabs[:, k, :], start=(k == 0), stop=(k == KT - 1))
            ins.then_inc(s_setp, 1)
            group_means(0, 1)
            pe.wait_ge(s_set, hops["wtot"])
            for t in range(CT):
                ins = MM(bank[1][:, t:t + 1], wtot[0:1, t * P:(t + 1) * P], ones[0:1, 0:1], start=True, stop=True)
            ins.then_inc(s_setp, 1)
            pe.wait_ge(s_set, hops["vdesc"])
            pe.wait_ge(s_poolset, 4)
            with pe.Fori(0, NCH) as j:
                feature_chunk(0, j, True)
            group_means(1, B)
            pe.wait_ge(s_qk, 1 + NCH)
            max_pass(0)
            with pe.Fori(0, B - 1) as b:
                attention(b)
                beside(layer1, b, feature_chunk)
                convolution(b, True)
            attention(B - 1)
            layer1(B - 1, nothing)
            convolution(B - 1, False)

        @block.gpsimd
        def _(pool):
            G = nc.gpsimd

            def pools(b, q, first, last):
                n = b * NCH + q
                nrow = ROWS + 2 - first - last
                pool.wait_ge(s_hx[0], 16 * CT * (n + 1 - NCH // 2))
                part(pool)
                for t in range(CT):
                    rowsx = hx[:, t, 0:nrow, :]
                    G.tensor_scalar(rowsx, rowsx, gcur[:, t, 0:1], gcur[:, t, 1:2], ALU.mult, ALU.add)\
                        .then_inc(s_norm, 1)
                pool.wait_ge(s_norm, CT * (n + 1))
                part(pool)
                link = chain(pool, s_pool, NCH * N_SUM0 + (n - NCH) * N_SUM + 2 * b + (0 if first else 1),
                             parted=True)
                windows(link, G, ALU.add, 0, first, last)

                def split(kind):
                    dst_h, dst_l = (c[:, kind * CT:(kind + 1) * CT, ts(q, CHUNK)] for c in (cath, catl))
                    link(G.tensor_copy(dst_h, pooled[kind][:]))
                    return G.tensor_tensor(dst_l, pooled[kind][:], dst_h, ALU.subtract)
                link(split(0))
                pool.wait_ge(s_maxp, n + 1)
                part(pool)
                split(1).then_inc(s_cat, 1)
                pool.wait_ge(s_cat, n + 1)
                part(pool)
                assert link.count == N_SUM + first + last, link.count

            def image(b):
                G.tensor_copy(gcur[:], gnp[:, b, :, 0:2]).then_inc(s_gcur, 1)
                pool.wait_ge(s_gcur, b)
                part(pool)
                pools(b, 0, 1, 0)
                with pool.Fori(1, NCH - 1) as q:
                    pools(b, q, 0, 0)
                pools(b, NCH - 1, 0, 1)

            for i, (dst, value) in enumerate(((threes[0][:], 0.0), (threes[1][:], -3.0e38),
                                              (ck[96:98, :], MAXROW), (vh[:, :, C:C + 1], 1.0))):
                G.memset(dst, value).then_inc(s_poolset, 1)
                pool.wait_ge(s_poolset, i + 1)

            def first_chunk(pair, odd, first, last):
                q = pair * 2 + odd
                pool.wait_ge(s_norm, CT * (q + 1))
                part(pool)
                windows(chain(pool, s_pool, q * N_SUM0 + 1 - first, parted=True), G, ALU.add, 0, first, last,
                        hxs[odd])
                pool.wait_ge(s_high, 2 * q + 2)
                part(pool)
                G.tensor_tensor(catl[:, 0:CT, ts(q, CHUNK)], pooled[0][:], cath[:, 0:CT, ts(q, CHUNK)],
                                ALU.subtract).then_inc(s_cat, 1)
                pool.wait_ge(s_cat, q + 1)
                part(pool)

            first_image(pool, first_chunk)
            pool.wait_ge(s_set, hops["gnp", 1])
            def stores_of(b):
                pool.wait_ge(s_usto, 16 * 5 * (b + 1))
                part(pool)
                load_kernels(pool, range(WIN - U_LOADS_POOL, WIN), s_uldp)
                with pool.Fori(0, NG // 2) as h:
                    for u in range(2):
                        store_y(pool, b, h * 2 + u, u, range(SP_STORES, Y_STORES), s_outp)

            with pool.Fori(1, B) as b:
                pool.wait_ge(s_vps, b * KEYT)
                part(pool)
                image(b)
                stores_of(b - 1)
            stores_of(B - 1)

        @block.sync
        def _(sp):
            for dst, src in ((cst_all[:], consts), (col[:], cols), (row[:], rows)):
                sp.dma_start(dst, src).then_inc(s_load, 16)
            sp.dma_start(wraw, wall).then_inc(s_wload, 16)
            for h in range(NCH // 2):
                sp.dma_start(x0[:, h], xv[0, :, :, ts(h, 2 * CHUNK)]).then_inc(s_x0[h], 16)

            def halo_rows(b, q, hx, s_loaded):
                r0 = max(0, ROWS * q - 1) if isinstance(q, int) else ROWS * q - 1
                n = ROWS + 1 if isinstance(q, int) and q in (0, NCH - 1) else ROWS + 2
                for t in range(CT):
                    sp.dma_start(hx[:, t, 0:n, :].rearrange("p r w -> p (r w)"),
                                 xv[b, :, t, ds(r0 * W, n * W)]).then_inc(s_loaded, 16)

            halo_rows(0, 0, hxs[0], s_hx[0])
            halo_rows(0, 1, hxs[1], s_hx[1])

            def first_chunk(pair, odd):
                q = pair * 2 + odd
                for image in range(1, B):
                    u, _, chunks = stat_chunk(pair, odd, image)
                    sp.wait_ge(s_xfree, chunks)
                    sp.dma_start(xin[:, u], xv[image, :, :, ts(q, CHUNK)]).then_inc(s_xin[u], 16)
                sp.wait_ge(s_cat, q + 1)
                sp.wait_ge(s_maxp, q + 1)
                if isinstance(q, int) and q + 2 >= NCH:
                    return
                halo_rows(0, q + 2, hxs[odd], s_hx[odd])

            with sp.Fori(0, NCH // 2 - 2) as h:
                first_chunk(h, 0)
                first_chunk(h, 1)
            for q in range(NCH - 4, NCH):
                first_chunk(q // 2, q % 2)
            for dst, src in ((w7s[:], w7), (wpws[:], wpw), (wa1s[:], wa1), (wa2s[:], wa2)):
                sp.dma_start(dst, src).then_inc(s_lload, 16)

            low = H + 3 - (NT - 1) * TO
            with sp.Fori(0, B) as b:
                for t in range(CT):
                    for win, a, z in ((0, 0, 3), (NT - 1, low, WIN)):
                        sp.dma_start(bass.AP(x1w, b * (NT * C * WIN * W) + (t * P * WIN * NT + a * NT + win) * W,
                                             [[WIN * NT * W, P], [NT * W, z - a], [1, W]]),
                                     zeros[:, 0:(z - a) * W]).then_inc(s_zero, 16)

            def halo_load(b, q):
                sp.wait_ge(s_cat, b * NCH + q)
                halo_rows(b, q, hx, s_hx[0])

            def store_x1(b, g):
                sp.wait_ge(s_x1, (b * NCH + g + 1) * CT)
                for t, a, z in pieces[g]:
                    k = a + 3 - TO * t
                    for ct in range(CT):
                        sp.dma_start(bass.AP(x1w, b * (NT * C * WIN * W) + (ct * P * WIN * NT + k * NT + t) * W,
                                             [[WIN * NT * W, P], [NT * W, z - a], [1, W]]),
                                     x1c[:, ct, (a - ROWS * g) * W:(z - ROWS * g) * W]).then_inc(s_x1o, 16)
                sp.wait_ge(s_x1o, 16 * (stores[NCH] * b + stores[g + 1]))
                part(sp)

            def attention(b, pool_next):
                for g in range(NCH):
                    if pool_next:
                        halo_load(b + 1, g)
                    if g:
                        store_x1(b, g - 1)
                    sp.dma_start(xin[:, 0], xv[b, :, :, ts(g, CHUNK)]).then_inc(s_xr, 16)
                store_x1(b, NCH - 1)

            def window_load(b, gi, u):
                sp.dma_start(xw[:, u], bass.AP(x1w, b * (NT * C * WIN * W) + gi * (GC * WIN * NT * W),
                                               [[NT * W, P], [W, NT], [1, W]])).then_inc(s_xw[u], 16)

            def layer1(b):
                for u in range(2):
                    window_load(b, u, u)
                sp.wait_ge(s_l1, N_L1 * b + hops["svec"])
                part(sp)
                for dst, v in ((scal_in, 0), (scal_out, 2)):
                    for t in range(CT):
                        sp.dma_start(bass.AP(dst, b * (GC * NG * 2) + t * (NG // CT) * 2,
                                             [[2, NG // CT], [NG * 2, GC], [1, 2]]),
                                     svec[:, t, v:v + 2]).then_inc(s_usto, 16)
                sp.wait_ge(s_usto, 16 * (5 * b + 4))
                part(sp)
                sp.dma_start(sin[:].rearrange("p g v -> p (g v)"),
                             bass.AP(scal_in, b * (GC * NG * 2), [[NG * 2, GC], [0, WIN], [1, NG * 2]]))\
                    .then_inc(s_uld, 16)
                sp.dma_start(sout[:].rearrange("p g v -> p (g v)"),
                             bass.AP(scal_out, b * (GC * NG * 2), [[0, TO], [NG * 2, GC], [1, NG * 2]]))\
                    .then_inc(s_uld, 16)
                sp.wait_ge(s_l1, N_L1 * (b + 1))
                part(sp)
                sp.dma_start(bass.AP(kern, 0, [[ULEN, P], [P * ULEN, CT], [1, ULEN]]), uker[:])\
                    .then_inc(s_usto, 16)
                sp.wait_ge(s_usto, 16 * 5 * (b + 1))
                load_kernels(sp, range(WIN - U_LOADS_POOL), s_uld)

            def convolution(b):
                def next_load(gi, u):
                    sp.wait_ge(s_xg, b * NG + gi + 1)
                    window_load(b, gi + 2, u)
                next_load(0, 0)
                with sp.Fori(0, NG // 2 - 2) as h:
                    for u in range(2):
                        next_load(h * 2 + u + 1, 1 - u)
                        store_y(sp, b, h * 2 + u, u, range(SP_STORES), s_out)
                next_load(NG - 3, 1)
                for gi in range(NG - 4, NG):
                    store_y(sp, b, gi, gi % 2, range(SP_STORES), s_out)
                for u in range(2):
                    sp.wait_ge(s_out[u], 16 * SP_STORES * (b + 1) * (NG // 2))
                    part(sp)
                    sp.wait_ge(s_outp[u], 16 * POOL_STORES * (b + 1) * (NG // 2))
                    part(sp)

            sp.wait_ge(s_zero, 16 * 4 * B)
            sp.wait_ge(s_xfree, 2 + (B - 1) * NCH)
            with sp.Fori(0, B - 1) as b:
                attention(b, True)
                layer1(b)
                convolution(b)
            attention(B - 1, False)
            layer1(B - 1)
            convolution(B - 1)
            for u in range(2):
                sp.wait_ge(s_out[u], 16 * SP_STORES * B * NG // 2)
                sp.wait_ge(s_outp[u], 16 * POOL_STORES * B * NG // 2)


def kernel(**inputs):
    import concourse.bacc as bacc
    from concourse.bass_utils import run_bass_kernel_spmd

    a = {k: np.asarray(v) for k, v in inputs.items()}

    def tiles(w):
        return np.ascontiguousarray(w.reshape(-1, P, w.shape[-1]).transpose(1, 0, 2))

    def vec(v):
        v = v.reshape(-1)
        if v.size < P:
            return np.pad(v, (0, P - v.size)).reshape(P, 1)
        return np.ascontiguousarray(v.reshape(-1, P).T)

    def kernel7(w):
        e = (TAPS - w.shape[-1]) // 2
        w = np.pad(w[:, 0], ((0, 0), (e, e), (e, e)))
        return np.ascontiguousarray(w.transpose(0, 2, 1)[:, :, ::-1]).reshape(C, 49)

    channel, shift = np.arange(P), np.abs(np.arange(7) - 3)
    groups = (channel[:, None] // GN_GROUP == channel[None] // GN_GROUP) / GN_GROUP
    at_row = TO * np.arange(NT)[None] + (channel % WIN)[:, None] - 3
    inside = (at_row >= 0) & (at_row < H)
    of_channel = channel[:, None] // WIN == np.arange(GC)[None]
    count = ((W - shift)[:, None] * (H - shift)[None]).reshape(1, 49)
    consts = np.concatenate([np.eye(P), groups, inside, of_channel], axis=1).astype(np.float32)

    w7 = np.stack([kernel7(a[f"L1_conv_w{k}"]) for k in (3, 5, 7)], axis=1)
    dwb = np.stack([vec(a[f"L1_conv_b{k}"]) for k in (3, 5, 7)], axis=2).reshape(P, 6)
    cols = np.concatenate([vec(a["L0_conv_bd"]), vec(a["L1_conv_b_pw"]), dwb,
                           vec(np.concatenate([a["L0_conv_bb"], a["L0_conv_bc"]])), vec(a["L1_conv_b_a1"])], axis=1)
    row = np.concatenate([a["L0_conv_bb"], a["L0_conv_bc"], a["L1_conv_b_a2"], a["L0_conv_alpha"].reshape(1),
                          count.astype(np.float32)[0]])
    arrays = {
        "x": a["x"].reshape(B, C, N),
        "wall": tiles(np.concatenate([a["L0_conv_wd"], a["L0_conv_wb"], a["L0_conv_wc"]]).T),
        "w7": tiles(w7.reshape(C, -1)).reshape(P, CT, 3, 49),
        "wpw": tiles(a["L1_conv_w_pw"].T),
        "wa1": tiles(a["L1_conv_w_a1"].T),
        "wa2": a["L1_conv_w_a2"].T,
        "cols": cols,
        "rows": np.broadcast_to(row, (P, row.size)),
        "consts": consts,
    }
    arrays = {k: np.ascontiguousarray(v) for k, v in arrays.items()}
    nc = bacc.Bacc("TRN2", target_bir_lowering=False, num_devices=1)
    aps = [nc.dram_tensor(k, v.shape, mybir.dt.from_np(v.dtype), kind="ExternalInput").ap()
           for k, v in arrays.items()]
    out = nc.dram_tensor("out", [B, C, N], F32, kind="ExternalOutput").ap()
    build(nc, *aps, out)
    r = run_bass_kernel_spmd(nc, [arrays], core_ids=[0])
    return r.results[0]["out"].reshape(B, C, H, W)
```
